# Optimizing a Trainium2 kernel written in Bass

```python
import numpy as np
import jax
import jax.numpy as jnp

def _softmax(x, axis=-1):
    return jax.nn.softmax(x, axis=axis)

def _gelu(x):
    return jax.nn.gelu(x, approximate=True)

def _silu(x):
    return jax.nn.silu(x)

def _sigmoid(x):
    return jax.nn.sigmoid(x)

def _layernorm(x, axis=-1, eps=1e-05):
    m = jnp.mean(x, axis=axis, keepdims=True)
    v = jnp.var(x, axis=axis, keepdims=True)
    return (x - m) / jnp.sqrt(v + eps)

def _scatter_add(tgt, idx, src, axis=0):
    return tgt.at[idx].add(src)

def _segment_sum(src, seg, n):
    return jax.ops.segment_sum(src, seg, n)
kernel_name = 'mk_decoder_postln_d1_seqx_r4_000eb5'

def setup_inputs(seed: int=0):
    np.random.seed(seed)
    _w = jnp.asarray

    def _rec_inputs():
        import jax
        import jax.numpy as jnp
        _rk = jax.random.key(seed)
        x = -0.0002928 + 1 * jax.random.normal(jax.random.fold_in(_rk, 1), (1, 2048, 256), jnp.float32)
        _lenS = 2048 - jax.random.randint(jax.random.fold_in(_rk, 7), (1,), 0, max(1, 2048 // 4) + 1, jnp.int32)
        _lenS2 = 1601 - jax.random.randint(jax.random.fold_in(_rk, 8), (1,), 0, max(1, 1601 // 4) + 1, jnp.int32)
        _ctx_1024P = jax.random.normal(jax.random.fold_in(_rk, 11), (1, 16, 256), jnp.float32)
        _ctx_1024c = jax.random.dirichlet(jax.random.fold_in(_rk, 511), 0.3 * jnp.ones((16,), jnp.float32), (1, 1601))
        _ctx_1024t = jnp.einsum('bsk,bkd->bsd', _ctx_1024c, _ctx_1024P)
        _ctx_1024t = _ctx_1024t * jax.lax.rsqrt(jnp.mean(jnp.square(_ctx_1024t)) + 1e-12) * 0.953939
        ctx_1024 = -1.39393e-06 + 0.999914 * (_ctx_1024t + 0.3 * jax.random.normal(jax.random.fold_in(_rk, 611), (1, 1601, 256), jnp.float32))
        return (x, ctx_1024)
    x, ctx_1024 = _rec_inputs()

    def _L0_attn_setup():
        import jax, jax.numpy as jnp
        import numpy as np
        B, N, QD = (4, 1024, 256)
        HEADS, DIM_HEAD = (8, 64)
        HID = HEADS * DIM_HEAD
        SCALE = DIM_HEAD ** (-0.5)
        key = jax.random.key(seed)
        ks = jax.random.split(key, 6)
        s_in = 1.0 / np.sqrt(QD)
        s_h = 1.0 / np.sqrt(HID)
        return {'x': jax.random.normal(ks[0], (B, N, QD), dtype=jnp.float32), 'Wq': jax.random.uniform(ks[1], (QD, HID), jnp.float32, -s_in, s_in), 'Wk': jax.random.uniform(ks[2], (QD, HID), jnp.float32, -s_in, s_in), 'Wv': jax.random.uniform(ks[3], (QD, HID), jnp.float32, -s_in, s_in), 'Wo': jax.random.uniform(ks[4], (HID, QD), jnp.float32, -s_h, s_h), 'bo': jax.random.uniform(ks[5], (QD,), jnp.float32, -s_h, s_h)}
    _L0_attn_all = _L0_attn_setup()
    _L0_attn_in = {k: v for k, v in _L0_attn_all.items() if k in ('Wq', 'Wk', 'Wv', 'Wo', 'bo')}
    del _L0_attn_all

    def _L0_xattn_setup():
        import jax, jax.numpy as jnp
        import numpy as np
        EMBED_DIM = 256
        NUM_HEADS = 16
        HEAD_DIM = EMBED_DIM // NUM_HEADS
        B, SQ, SK = (2, 512, 512)
        key = jax.random.key(seed)
        ks = jax.random.split(key, 11)
        s = 1.0 / np.sqrt(EMBED_DIM)
        return {'query': jax.random.normal(ks[0], (B, SQ, EMBED_DIM), jnp.float32), 'key': jax.random.normal(ks[1], (B, SK, EMBED_DIM), jnp.float32), 'value': jax.random.normal(ks[2], (B, SK, EMBED_DIM), jnp.float32), 'Wq': jax.random.normal(ks[3], (EMBED_DIM, EMBED_DIM), jnp.float32) * s, 'bq': jnp.zeros((EMBED_DIM,), jnp.float32), 'Wk': jax.random.normal(ks[4], (EMBED_DIM, EMBED_DIM), jnp.float32) * s, 'bk': jnp.zeros((EMBED_DIM,), jnp.float32), 'Wv': jax.random.normal(ks[5], (EMBED_DIM, EMBED_DIM), jnp.float32) * s, 'bv': jnp.zeros((EMBED_DIM,), jnp.float32), 'Wo': jax.random.normal(ks[6], (EMBED_DIM, EMBED_DIM), jnp.float32) * s, 'bo': jnp.zeros((EMBED_DIM,), jnp.float32)}
    _L0_xattn_all = _L0_xattn_setup()
    _L0_xattn_in = {k: v for k, v in _L0_xattn_all.items() if k in ('Wq', 'bq', 'Wk', 'bk', 'Wv', 'bv', 'Wo', 'bo')}
    del _L0_xattn_all

    def _L0_ffn_setup():
        import jax, jax.numpy as jnp
        import numpy as np
        DIM = 256
        HID = 128
        N_EXPERTS = 16
        TOP_K = 4
        key = jax.random.key(seed)
        ks = jax.random.split(key, 8)
        s = 0.02
        x = jax.random.normal(ks[0], (2, 256, DIM), dtype=jnp.float32)
        gate_w = jax.random.normal(ks[1], (N_EXPERTS, DIM), dtype=jnp.float32) * s
        w1 = jax.random.normal(ks[2], (N_EXPERTS, HID, DIM), dtype=jnp.float32) * s
        w3 = jax.random.normal(ks[3], (N_EXPERTS, HID, DIM), dtype=jnp.float32) * s
        w2 = jax.random.normal(ks[4], (N_EXPERTS, DIM, HID), dtype=jnp.float32) * s
        sw1 = jax.random.normal(ks[5], (HID, DIM), dtype=jnp.float32) * s
        sw3 = jax.random.normal(ks[6], (HID, DIM), dtype=jnp.float32) * s
        sw2 = jax.random.normal(ks[7], (DIM, HID), dtype=jnp.float32) * s
        return {'x': x, 'gate_w': gate_w, 'w1': w1, 'w3': w3, 'w2': w2, 'sw1': sw1, 'sw3': sw3, 'sw2': sw2}
    _L0_ffn_all = _L0_ffn_setup()
    _L0_ffn_in = {k: v for k, v in _L0_ffn_all.items() if k in ('gate_w', 'w1', 'w3', 'w2', 'sw1', 'sw3', 'sw2')}
    del _L0_ffn_all
    return {'x': x, 'ctx_1024': ctx_1024, 'L0_attn_Wq': _L0_attn_in['Wq'], 'L0_attn_Wk': _L0_attn_in['Wk'], 'L0_attn_Wv': _L0_attn_in['Wv'], 'L0_attn_Wo': _L0_attn_in['Wo'], 'L0_attn_bo': _L0_attn_in['bo'], 'L0_xattn_Wq': _L0_xattn_in['Wq'], 'L0_xattn_bq': _L0_xattn_in['bq'], 'L0_xattn_Wk': _L0_xattn_in['Wk'], 'L0_xattn_bk': _L0_xattn_in['bk'], 'L0_xattn_Wv': _L0_xattn_in['Wv'], 'L0_xattn_bv': _L0_xattn_in['bv'], 'L0_xattn_Wo': _L0_xattn_in['Wo'], 'L0_xattn_bo': _L0_xattn_in['bo'], 'L0_ffn_gate_w': _L0_ffn_in['gate_w'], 'L0_ffn_w1': _L0_ffn_in['w1'], 'L0_ffn_w3': _L0_ffn_in['w3'], 'L0_ffn_w2': _L0_ffn_in['w2'], 'L0_ffn_sw1': _L0_ffn_in['sw1'], 'L0_ffn_sw3': _L0_ffn_in['sw3'], 'L0_ffn_sw2': _L0_ffn_in['sw2']}

def reference(x, ctx_1024, L0_attn_Wq, L0_attn_Wk, L0_attn_Wv, L0_attn_Wo, L0_attn_bo, L0_xattn_Wq, L0_xattn_bq, L0_xattn_Wk, L0_xattn_bk, L0_xattn_Wv, L0_xattn_bv, L0_xattn_Wo, L0_xattn_bo, L0_ffn_gate_w, L0_ffn_w1, L0_ffn_w3, L0_ffn_w2, L0_ffn_sw1, L0_ffn_sw3, L0_ffn_sw2):
    import jax
    import jax.numpy as jnp

    def _L0_attn_ref(x, Wq, Wk, Wv, Wo, bo):
        import jax, jax.numpy as jnp
        import numpy as np
        B, N, QD = (4, 1024, 256)
        HEADS, DIM_HEAD = (8, 64)
        HID = HEADS * DIM_HEAD
        SCALE = DIM_HEAD ** (-0.5)
        b, n, _ = x.shape
        q = x @ Wq
        k = x @ Wk
        v = x @ Wv

        def split_heads(t):
            return t.reshape(b, n, HEADS, DIM_HEAD).transpose(0, 2, 3, 1)
        q = split_heads(q)
        k = split_heads(k)
        v = split_heads(v)
        q = jax.nn.softmax(q, axis=-2) * SCALE
        k = jax.nn.softmax(k, axis=-1)
        context = jnp.einsum('bhdn,bhen->bhde', k, v)
        out = jnp.einsum('bhde,bhdn->bhen', context, q)
        out = out.transpose(0, 3, 1, 2).reshape(b, n, HID)
        return out @ Wo + bo

    def _L0_xattn_ref(query, key, value, Wq, bq, Wk, bk, Wv, bv, Wo, bo):
        import jax, jax.numpy as jnp
        import numpy as np
        EMBED_DIM = 256
        NUM_HEADS = 16
        HEAD_DIM = EMBED_DIM // NUM_HEADS
        B, SQ, SK = (2, 512, 512)
        b, sq, _ = query.shape
        sk = key.shape[1]
        Q = (query @ Wq + bq).reshape(b, sq, NUM_HEADS, HEAD_DIM).transpose(0, 2, 1, 3)
        K = (key @ Wk + bk).reshape(b, sk, NUM_HEADS, HEAD_DIM).transpose(0, 2, 1, 3)
        V = (value @ Wv + bv).reshape(b, sk, NUM_HEADS, HEAD_DIM).transpose(0, 2, 1, 3)
        scale = 1.0 / np.sqrt(HEAD_DIM)
        scores = jnp.einsum('bhqd,bhkd->bhqk', Q, K) * scale
        attn = jax.nn.softmax(scores, axis=-1)
        out = jnp.einsum('bhqk,bhkd->bhqd', attn, V)
        out = out.transpose(0, 2, 1, 3).reshape(b, sq, EMBED_DIM)
        return out @ Wo + bo

    def _L0_ffn_ref(x, gate_w, w1, w3, w2, sw1, sw3, sw2):
        import jax, jax.numpy as jnp
        import numpy as np
        DIM = 256
        HID = 128
        N_EXPERTS = 16
        TOP_K = 4
        bsz, seq_len, dim = x.shape
        xf = x.reshape(-1, dim)
        T = xf.shape[0]
        probs = jax.nn.softmax(xf @ gate_w.T, axis=-1)
        top_w, top_idx = jax.lax.top_k(probs, TOP_K)
        top_w = top_w / jnp.sum(top_w, axis=-1, keepdims=True)
        rows = jnp.arange(T)[:, None]
        combine = jnp.zeros((T, N_EXPERTS), dtype=xf.dtype).at[rows, top_idx].set(top_w)
        h1 = jnp.einsum('td,ehd->teh', xf, w1)
        h3 = jnp.einsum('td,ehd->teh', xf, w3)
        act = jax.nn.silu(h1) * h3
        eout = jnp.einsum('teh,edh->ted', act, w2)
        moe_out = jnp.einsum('ted,te->td', eout, combine)
        shared = jax.nn.silu(xf @ sw1.T) * (xf @ sw3.T) @ sw2.T
        return (moe_out + shared).reshape(bsz, seq_len, dim)
    x = _layernorm(x + _L0_attn_ref(x, L0_attn_Wq, L0_attn_Wk, L0_attn_Wv, L0_attn_Wo, L0_attn_bo), axis=-1)
    x = _layernorm(x + _L0_xattn_ref(x, ctx_1024, ctx_1024, L0_xattn_Wq, L0_xattn_bq, L0_xattn_Wk, L0_xattn_bk, L0_xattn_Wv, L0_xattn_bv, L0_xattn_Wo, L0_xattn_bo), axis=-1)
    x = _layernorm(x + _L0_ffn_ref(x, L0_ffn_gate_w, L0_ffn_w1, L0_ffn_w3, L0_ffn_w2, L0_ffn_sw1, L0_ffn_sw3, L0_ffn_sw2), axis=-1)
    return x

_drawn_inputs = setup_inputs


def setup_inputs(seed=0):
    import zlib

    import numpy as np

    out = dict(_drawn_inputs(seed))
    spreads = {'L0_xattn_bq': (0.0, 0.407),
     'L0_xattn_bk': (0.0, 0.8),
     'L0_xattn_bv': (0.0, 0.1),
     'L0_xattn_bo': (0.0, 0.1)}
    factors = {'L0_attn_Wq': 8.0,
     'L0_attn_Wk': 8.0,
     'L0_attn_Wv': 8.0,
     'L0_attn_Wo': 8.0,
     'L0_ffn_gate_w': 8.0,
     'L0_ffn_w1': 8.0,
     'L0_ffn_w3': 8.0,
     'L0_ffn_w2': 8.0,
     'L0_ffn_sw1': 4.374,
     'L0_ffn_sw3': 4.38,
     'L0_ffn_sw2': 4.22}
    for name, (base, spread) in spreads.items():
        noise = np.random.default_rng([zlib.crc32(name.encode()), seed]).standard_normal(out[name].shape)
        drawn = base * np.exp(spread * noise) if base else spread * noise
        out[name] = jnp.asarray(drawn.astype(out[name].dtype))
    for name, factor in factors.items():
        out[name] = (out[name] * factor).astype(out[name].dtype)
    return out
```

```python
from contextlib import ExitStack

import concourse.bass as bass
from concourse import mybir

F32 = mybir.dt.float32
BF16 = mybir.dt.bfloat16
ALU = mybir.AluOpType
ACT = mybir.ActivationFunctionType
X = mybir.AxisListType.X

P = 128
SEQ, DIM = 2048, 256
KEYS = 1601
TILES = SEQ // P
CHUNK = 512
CHUNKS = SEQ // CHUNK
TPC = CHUNK // P
DK = DIM // P
S_HEADS, S_DH = 8, 64
S_HID = S_HEADS * S_DH
SF = S_HID // P
S_SCALE = S_DH ** -0.5
C_HEADS, C_DH = 16, 16
C_SCALE = C_DH ** -0.5
GROUP = 4
GROUPS = C_HEADS // GROUP
KT = -(-KEYS // P)
LASTK = KEYS - (KT - 1) * P
VW = P // GROUP
SPLIT = 6
LEVELS = 3
SROWS = SPLIT * C_DH
Q_LEVEL = (0, 0, 0, 1, 1, 2)
K_LEVEL = (0, 1, 2, 0, 1, 0)
PIECES = 4
PW = -(-KEYS // PIECES)
UNITS = TPC * GROUP * PIECES
SPLIT_STEPS = 6
LEAD = KT + 4
EXPERTS, HID, TOPK = 16, 128, 4
FFN = EXPERTS + 1
EPS = 1e-5


def krows(kt):
    return P if kt < KT - 1 else LASTK


def piece(n):
    at = 0 if n == 0 else PW + (n - 1) * (PW - 1)
    return at, PW if n == 0 else PW - 1


assert sum(piece(n)[1] for n in range(PIECES)) == KEYS and LASTK > 0


def decoder_layer(nc, a, out):
    with ExitStack() as ctx:
        def sb(name, shape, dt=F32):
            return ctx.enter_context(nc.sbuf_tensor(name, shape, dt))

        def sem(name):
            return ctx.enter_context(nc.semaphore(name))

        kparts_d = nc.dram_tensor("kparts_d", (LEVELS, DIM, KEYS), BF16).ap()
        qparts_d = nc.dram_tensor("qparts_d", (LEVELS, DIM, SEQ), BF16).ap()

        psum = ctx.enter_context(nc.psum_tensor("psum", [P, 8 * CHUNK], F32))

        def bank(n, w=1):
            return psum[:, n * CHUNK:(n + w) * CHUNK]

        MAX_BANKS = (3, 6, 7)
        ST_BANKS = 3

        x_sb = sb("x_sb", [P, TILES, DIM])
        xT = sb("xT", [P, DK, SEQ])
        numT = sb("numT", [P, CHUNK])
        attn = sb("attn", [P, TPC, GROUPS, GROUP, C_DH])
        attnT = sb("attnT", [P, DK, CHUNK])
        wo_c = sb("wo_c", [P, DK, DIM])
        den_rec = sb("den_rec", [P, TPC, GROUP, 1])
        ident = sb("ident", [P, P])
        ident_b = sb("ident_b", [P, P], BF16)
        half_neg = sb("half_neg", [P, TPC])
        stats = sb("stats", [P, TPC, 6])
        meanvar = sb("meanvar", [P, TPC, 2])
        var_eps = sb("var_eps", [P, TPC])
        rstd = sb("rstd", [P, TPC])
        bq_c = sb("bq_c", [P, DK])
        bk_c = sb("bk_c", [P, DK])
        small = sb("small", [P, 64])
        mpart = sb("mpart", [P, 2, TPC * GROUP, PIECES])
        negmax = sb("negmax", [P, TPC * GROUP])
        nres = sb("nres", [P, TPC * GROUP])
        mlev = sb("mlev", [P, TPC, LEVELS, GROUP], BF16)
        maxT = sb("maxT", [LEVELS * GROUP, 2, CHUNK], BF16)

        region1 = sb("region1", [P, C_HEADS * (KEYS + 1) // 2 + KT * C_HEADS * VW])
        ekT = region1[:, 0:SF * SEQ].rearrange("p (f n) -> p f n", f=SF)
        v_s = region1[:, SF * SEQ:2 * SF * SEQ].rearrange("p (t n) -> p t n", t=TILES)
        KW = C_HEADS * KEYS // 2
        kstack = region1[:, 0:KW].bitcast(BF16).rearrange("p (h n) -> p h n", h=C_HEADS)
        vals = region1[:, KW:KW + KT * C_HEADS * VW].rearrange("p (t h w) -> p t h w", t=KT, h=C_HEADS)

        region2 = sb("region2", [P, 4 * CHUNK // 2 * GROUP + 3 * GROUP * CHUNK])

        def r2(at, n):
            return region2[:, at:at + n]

        ek = r2(0, TILES * CHUNK).rearrange("p (t n) -> p t n", t=TILES)
        context = r2(TILES * CHUNK, SF * P).rearrange("p (f n) -> p f n", f=SF)
        kf = r2(0, DK * KEYS).rearrange("p (f n) -> p f n", f=DK)
        kres = r2(DK * KEYS, KEYS)
        kpart = r2(3 * KEYS + 1, 3 * KEYS + 3).bitcast(BF16)[:, 0:DK * LEVELS * KEYS].rearrange(
            "p (k f n) -> p k f n", k=LEVELS, f=DK)
        qexp = r2(0, 2 * S_HID).rearrange("p (b n) -> p b n", b=2)
        qnorm = r2(1024, 2 * S_HID).rearrange("p (b n) -> p b n", b=2)
        qsT = r2(2048, 2 * S_HID).rearrange("p (b n) -> p b n", b=2)
        resid = r2(3072, 2 * DIM).rearrange("p (b n) -> p b n", b=2)
        qf = r2(3584, DK * CHUNK)
        qres = r2(4608, DK * CHUNK)
        qpart = r2(5632, LEVELS * DK * CHUNK // 2).bitcast(BF16).rearrange("p (k n) -> p k n", k=LEVELS)
        qstack = r2(0, 4 * GROUP * CHUNK // 2).bitcast(BF16).rearrange("p (b h n) -> p b h n", b=4, h=GROUP)
        prob = r2(4096, 3 * GROUP * CHUNK).rearrange("p (b h n) -> p b h n", b=3, h=GROUP)
        w2T = r2(0, FFN * DIM).rearrange("p (e n) -> p e n", e=FFN)
        tanh_h = r2(4352, 2 * CHUNK).rearrange("p (b n) -> p b n", b=2)
        silu_h = r2(5376, CHUNK)
        hprod = r2(5888, CHUNK)
        act_h = r2(6400, 2 * CHUNK).rearrange("p (b n) -> p b n", b=2)
        ffnT = r2(7424, DK * CHUNK).rearrange("p (d n) -> p d n", d=DK)

        region3 = sb("region3", [P, 4 * 1024 + 1024 + DK * KEYS + 3 * DK * DIM])

        def r3(at, n, **k):
            return region3[:, at:at + n]

        wq_s, wk_s, wv_s = (r3(1024 * n, 1024).rearrange("p (k n) -> p k n", k=DK) for n in range(3))
        wo_s = r3(3072, 1024).rearrange("p (f n) -> p f n", f=SF)
        fold = r3(4096, 1024).rearrange("p (f n) -> p f n", f=SF)
        ctxT = r3(5120, DK * KEYS).rearrange("p (k n) -> p k n", k=DK)
        wq_c, wk_c, wv_c = (r3(5120 + DK * KEYS + 512 * n, 512).rearrange("p (k n) -> p k n", k=DK)
                            for n in range(3))
        w1T = r3(0, DK * FFN * HID).rearrange("p (k e n) -> p k e n", k=DK, e=FFN)
        w3T = r3(DK * FFN * HID, DK * FFN * HID).rearrange("p (k e n) -> p k e n", k=DK, e=FFN)

        bo_row = sb("bo_row", [P, DIM])
        bv_row = sb("bv_row", [P, DIM])
        boc_row = sb("boc_row", [P, DIM])
        nkmax = sb("nkmax", [P, SF])
        ksum = sb("ksum", [P, SF])
        krec = sb("krec", [P, SF])
        gate_wT = sb("gate_wT", [P, DK, EXPERTS])
        GW = TILES * EXPERTS

        def gate_tile(n):
            return region1[:, n * GW:(n + 1) * GW].rearrange("p (t e) -> p t e", t=TILES)

        probs, zero_gate, gate_work, gate_equal, gate_count = (gate_tile(n) for n in range(5))
        top8 = sb("top8", [P, TILES, 8])
        cT = region1[0:EXPERTS, 5 * GW:5 * GW + SEQ]
        expert_sel = region1[0:EXPERTS, 5 * GW + SEQ:5 * GW + SEQ + EXPERTS * P].rearrange(
            "p (e n) -> p e n", e=EXPERTS)

        def sems(*names):
            return [sem(n) for n in names]

        ld_xT, ld_wk, ld_wv, ld_wq, ld_wo, ld_x, ld_ctx, ld_cw, ld_bias, ld_woc = sems(
            "ld_xT", "ld_wk", "ld_wv", "ld_wq", "ld_wo", "ld_x", "ld_ctx", "ld_cw", "ld_bias", "ld_woc")
        (consts_ready, zeros_ready, x_biased, kT_ready, kmax_ready, k_exp, v_ready, v_copied, ekT_ready,
         ek_copied, ctx_ready, ctx_copied, fold_ready, fold_copied) = sems(
            "consts_ready", "zeros_ready", "x_biased", "kT_ready", "kmax_ready", "k_exp", "v_ready",
            "v_copied", "ekT_ready", "ek_copied", "ctx_ready", "ctx_copied", "fold_ready", "fold_copied")
        kc_ready, kc_copied, k_split, k_written, k_stacked, vc_ready, vc_copied = sems(
            "kc_ready", "kc_copied", "k_split", "k_written", "k_stacked", "vc_ready", "vc_copied")
        (q_ready, q_centred, q_exp, qn_ready, qT_ready, qT_copied, y_ready, y_read, b_var, b_rstd,
         x1_ready, x1T_ready, x1T_copied, qp_ready, qf_copied, q_split, q_written) = sems(
            "q_ready", "q_centred", "q_exp", "qn_ready", "qT_ready", "qT_copied", "y_ready", "y_read",
            "b_var", "b_rstd", "x1_ready", "x1T_ready", "x1T_copied", "qp_ready", "qf_copied", "q_split",
            "q_written")
        q_stacked = sems(*(f"q_stacked{g}" for g in range(GROUPS)))
        (max_scores, max_read, max_split, maxT_ready, maxT_copied, max_stacked, st_ready, p_ready,
         pv_done, num_copied, den_ready, attn_ready, co_ready, co_read, c_var, c_rstd, x2_ready, x2T_ready,
         x2T_copied) = sems(
            "max_scores", "max_read", "max_split", "maxT_ready", "maxT_copied", "max_stacked",
            "st_ready", "p_ready", "pv_done", "num_copied", "den_ready", "attn_ready", "co_ready", "co_read",
            "c_var", "c_rstd", "x2_ready", "x2T_ready", "x2T_copied")
        gate_centred, gate_exp = sems("gate_centred", "gate_exp")
        sel_ready, x1_biased, attnT_ready, attnT_copied = sems("sel_ready", "x1_biased", "attnT_ready", "attnT_copied")
        (ld_w1, ld_w2, logits_ready, combine_ready, cT_ready, cT_copied, h_ready, tanh_ready, h_read, cb_ready,
         gated, act_done, ffn_copied, ffnN_ready, ffnN_read, d_var, d_rstd, out_ready, out_written) = sems(
            "ld_w1", "ld_w2", "logits_ready", "combine_ready", "cT_ready", "cT_copied", "h_ready", "tanh_ready",
            "h_read", "cb_ready", "gated", "act_done", "ffn_copied", "ffnN_ready", "ffnN_read",
            "d_var", "d_rstd", "out_ready", "out_written")
        vec_step = sem("vec_step")
        pool_step = sem("pool_step")

        block = ctx.enter_context(nc.Block())

        def units_until(step):
            return min(CHUNKS * GROUPS * UNITS, -(-UNITS * (step + 1 + LEAD) // KT))

        STEPS = CHUNKS * GROUPS * KT

        @block.sync
        def _(sp):
            sp.dma_start(xT[:, :, :], a["xT"].rearrange("(k p) n -> p k n", p=P)).then_inc(ld_xT, 16)
            sp.dma_start(wv_s, a["L0_attn_Wv"].rearrange("(k p) n -> p k n", p=P)).then_inc(ld_wv, 16)
            sp.dma_start(ctxT, a["ctxT"].rearrange("(k p) n -> p k n", p=P)).then_inc(ld_ctx, 16)
            sp.dma_start(wq_s, a["L0_attn_Wq"].rearrange("(k p) n -> p k n", p=P)).then_inc(ld_wq, 16)
            for w, name in ((wq_c, "L0_xattn_Wq"), (wk_c, "L0_xattn_Wk"), (wv_c, "L0_xattn_Wv")):
                sp.dma_start(w, a[name].rearrange("(k p) n -> p k n", p=P)).then_inc(ld_cw, 16)
            sp.dma_start(wo_c[:, :, :], a["L0_xattn_Wo"].rearrange("(k p) n -> p k n", p=P)).then_inc(ld_woc, 16)
            sp.wait_ge(k_split, 1)
            for k in range(LEVELS):
                sp.dma_start(kparts_d[k].rearrange("(f p) n -> p f n", p=P), kpart[:, k]).then_inc(k_written, 16)
            sp.wait_ge(k_written, 16 * LEVELS)
            for b in range(SPLIT):
                sp.dma_start(kstack[C_DH * b:C_DH * b + C_DH, :, :],
                             kparts_d[K_LEVEL[b]].rearrange("(h d) n -> d h n", d=C_DH)).then_inc(k_stacked, 16)
            for c in range(CHUNKS):
                sp.wait_ge(q_split, c + 1)
                sp.dma_start(qparts_d[:, :, c * CHUNK:(c + 1) * CHUNK].rearrange("k (f p) n -> p (k f) n", p=P),
                             qpart.rearrange("p k (f n) -> p (k f) n", f=DK)).then_inc(q_written, 16)
            sp.wait_ge(qp_ready, CHUNKS)
            sp.wait_ge(vc_ready, KT)
            for w, name, shared in ((w1T, "w1T", "sw1T"), (w3T, "w3T", "sw3T")):
                for k in range(DK):
                    sp.dma_start(w[:, k, 0:EXPERTS, :], a[name][k * P:(k + 1) * P]).then_inc(ld_w1, 16)
                    sp.dma_start(w[:, k, EXPERTS, :], a[shared][k * P:(k + 1) * P, :]).then_inc(ld_w1, 16)

            def stack_queries(G):
                c, g = divmod(G, GROUPS)
                if G == 0:
                    sp.wait_ge(q_written, 16 * CHUNKS)
                if G >= 4:
                    sp.wait_ge(st_ready, GROUP * KT * (G - 3))
                for b in range(SPLIT):
                    sp.dma_start(
                        qstack[C_DH * b:C_DH * b + C_DH, g, :, :],
                        qparts_d[Q_LEVEL[b], g * GROUP * C_DH:(g + 1) * GROUP * C_DH,
                                 c * CHUNK:(c + 1) * CHUNK].rearrange("(h d) n -> d h n", d=C_DH)
                    ).then_inc(q_stacked[g], 16)

            def stack_max(G):
                sp.wait_ge(maxT_copied, G + 1)
                for k in range(LEVELS):
                    sp.dma_start(qstack[SROWS + k:SROWS + k + 1, G % GROUPS, :, :],
                                 maxT[GROUP * k:GROUP * k + GROUP, G % 2, :]).then_inc(max_stacked, 16)

            n = CHUNKS * GROUPS
            for G in range(n + 2):
                if G < n:
                    stack_queries(G)
                if G >= 2:
                    stack_max(G - 2)
            sp.wait_ge(pv_done, STEPS)
            sp.wait_ge(st_ready, GROUP * STEPS)
            sp.dma_start(w2T[:, 0:EXPERTS, :], a["w2T"]).then_inc(ld_w2, 16)
            sp.dma_start(w2T[:, EXPERTS, :], a["sw2T"]).then_inc(ld_w2, 16)
            for t in range(TILES):
                sp.wait_ge(out_ready, t + 1)
                sp.dma_start(out[t * P:(t + 1) * P, :], x_sb[:, t, :]).then_inc(out_written, 16)
            sp.wait_ge(out_written, 16 * TILES)

        @block.gpsimd
        def _(pool):
            n = [0]

            def link(ins):
                n[0] += 1
                ins.then_inc(pool_step, 1)
                pool.wait_ge(pool_step, n[0])

            pool.memset(context, 0.0).then_inc(zeros_ready, 1)
            link(pool.memset(ident[:, :], 0.0))
            link(pool.memset(half_neg[:, :], -0.5))
            link(pool.affine_select(out=ident[:, :], in_=ident[:, :], compare_op=ALU.not_equal, fill=1.0,
                                    base=0, pattern=[[-1, P]], channel_multiplier=1))
            pool.tensor_copy(ident_b[:, :], ident[:, :]).then_inc(consts_ready, 1)
            pool.wait_ge(ld_x, 16)
            pool.wait_ge(ld_bias, 16 * 7)
            for t in range(TILES):
                pool.tensor_tensor(x_sb[:, t, :], x_sb[:, t, :], bo_row[:, :], ALU.add).then_inc(x_biased, 1)
            pool.wait_ge(ctx_ready, 1)
            link(pool.memset(vals, 0.0))
            pool.memset(vals[:, :, :, C_DH:C_DH + 1], 1.0).then_inc(zeros_ready, 1)
            pool.wait_ge(zeros_ready, 2)
            pool.memset(region1[SROWS:SROWS + LEVELS, 0:KW], 1.0 + 0x3F80 * 2.0 ** -23).then_inc(zeros_ready, 1)
            pool.wait_ge(zeros_ready, 3)
            for var, done, count, w in ((b_var, b_rstd, TILES, 1), (c_var, c_rstd, CHUNKS, TPC),
                                        (d_var, d_rstd, CHUNKS, TPC)):
                for t in range(count):
                    if var is c_var and t == 0:
                        for n_t in range(TILES):
                            pool.wait_ge(x1T_ready, n_t + 1)
                            pool.tensor_tensor(x_sb[:, n_t, :], x_sb[:, n_t, :], boc_row[:, :],
                                               ALU.add).then_inc(x1_biased, 1)
                    if var is c_var and t == CHUNKS - 1:
                        pool.wait_ge(pv_done, STEPS)
                        link(pool.memset(zero_gate, 0.0))
                        link(pool.memset(expert_sel, 0.0))
                        pool.affine_select(out=expert_sel, in_=expert_sel, compare_op=ALU.not_equal, fill=1.0,
                                           base=0, pattern=[[-1, EXPERTS], [0, P]],
                                           channel_multiplier=1).then_inc(sel_ready, 1)
                    pool.wait_ge(var, t + 1)
                    at = t % TPC if w == 1 else 0
                    pool.tensor_tensor(rstd[:, at:at + w], var_eps[:, at:at + w], half_neg[:, 0:w],
                                       ALU.pow).then_inc(done, 1)

        @block.scalar
        def _(act):
            act.dma_start(wk_s, a["L0_attn_Wk"].rearrange("(k p) n -> p k n", p=P)).then_inc(ld_wk, 16)
            act.dma_start(x_sb[:, :, :], a["x"].rearrange("(t p) n -> p t n", p=P)).then_inc(ld_x, 16)
            act.dma_start(wo_s, a["L0_attn_Wo"].rearrange("(f p) n -> p f n", p=P)).then_inc(ld_wo, 16)
            act.dma_start(bo_row[:, :], a["L0_attn_bo"].rearrange("(a n) -> a n", a=1).broadcast_to([P, DIM])).then_inc(ld_bias, 16)
            act.dma_start(bv_row[:, :], a["L0_xattn_bv"].rearrange("(a n) -> a n", a=1).broadcast_to([P, DIM])).then_inc(ld_bias, 16)
            act.dma_start(boc_row[:, :], a["L0_xattn_bo"].rearrange("(a n) -> a n", a=1).broadcast_to([P, DIM])).then_inc(ld_bias, 16)
            act.dma_start(bq_c[:, :], a["bq2"]).then_inc(ld_bias, 16)
            act.dma_start(bk_c[:, :], a["bk2"]).then_inc(ld_bias, 16)
            for k in range(DK):
                act.dma_start(gate_wT[:, k, :], a["gateT"][k * P:(k + 1) * P, :]).then_inc(ld_bias, 16)

            for f in range(SF):
                act.wait_ge(kmax_ready, f + 1)
                act.activation(ekT[:, f, :], bank(4 * (f % 2), 4), ACT.Exp, bias=nkmax[:, f:f + 1],
                               accum_out=ksum[:, f:f + 1]).then_inc(k_exp, 1)
            for t in range(TILES):
                act.wait_ge(ekT_ready, t + 1)
                act.activation(ek[:, t, :], bank(4 + t % 2), ACT.Copy).then_inc(ek_copied, 1)
            act.wait_ge(ld_bias, 16 * 7)
            for f in range(DK):
                act.wait_ge(kc_ready, f + 1)
                act.activation(kf[:, f, :], psum[:, 4 * f * CHUNK:4 * f * CHUNK + KEYS], ACT.Identity,
                               bias=bk_c[:, f:f + 1]).then_inc(kc_copied, 1)

            for i in range(TILES + 13):
                if i < TILES:
                    act.wait_ge(q_centred, i + 1)
                    act.activation(qexp[:, i % 2, :], qexp[:, i % 2, :], ACT.Exp).then_inc(q_exp, 1)
                t = i - 2
                if 0 <= t < TILES:
                    act.wait_ge(qT_ready, t + 1)
                    if t >= 2:
                        act.wait_ge(y_ready, t - 1)
                    act.activation(qsT[:, t % 2, :], bank(2 + t % 2), ACT.Copy).then_inc(qT_copied, 1)
                t = i - 6
                if 0 <= t < TILES:
                    act.wait_ge(x1T_ready, t + 1)
                    act.activation(xT[:, :, t * P:(t + 1) * P],
                                   bank(5)[:, 0:DK * P].rearrange("p (k n) -> p k n", k=DK),
                                   ACT.Copy).then_inc(x1T_copied, 1)
                if (i - 11) % TPC == 0 and 0 <= (i - 11) // TPC < CHUNKS:
                    c = (i - 11) // TPC
                    act.wait_ge(qp_ready, c + 1)
                    if c >= 1:
                        act.wait_ge(q_split, c)
                    for f in range(DK):
                        act.activation(qf[:, f * CHUNK:(f + 1) * CHUNK], bank(6 + f), ACT.Identity,
                                       bias=bq_c[:, f:f + 1]).then_inc(qf_copied, 1)

            def copy_max(G):
                act.wait_ge(maxT_ready, G + 1)
                if G >= 2:
                    act.wait_ge(max_stacked, 16 * LEVELS * (G - 1))
                act.activation(maxT[:, G % 2, :], bank(5).bitcast(BF16)[0:LEVELS * GROUP, 0:CHUNK],
                               ACT.Copy).then_inc(maxT_copied, 1)

            def copy_num(G):
                act.wait_ge(pv_done, KT * (G + 1))
                if G >= 1:
                    act.wait_ge(den_ready, G)
                act.activation(numT[:, :], bank(4), ACT.Copy).then_inc(num_copied, 1)

            def copy_attnT(c, k):
                act.wait_ge(attnT_ready, DK * c + k + 1)
                if c >= 1:
                    act.wait_ge(co_ready, 2 * c)
                act.activation(attnT[:, k, :], bank(5), ACT.Copy).then_inc(attnT_copied, 1)

            def copy_x2T(c, k):
                act.wait_ge(x2T_ready, DK * c + k + 1)
                act.activation(xT[:, k, c * CHUNK:(c + 1) * CHUNK], bank(5), ACT.Copy).then_inc(x2T_copied, 1)

            copy_max(0)
            for G in range(CHUNKS * GROUPS):
                c, g = divmod(G, GROUPS)
                for kt in range(KT):
                    s = KT * G + kt
                    r = krows(kt)
                    if s >= 3:
                        act.wait_ge(pv_done, s - 2)
                    for j in range(GROUP):
                        n = GROUP * s + j
                        act.wait_ge(st_ready, n + 1)
                        act.activation(prob[0:r, s % 3, j, :], bank(n % ST_BANKS)[0:r],
                                       ACT.Exp).then_inc(p_ready, 1)
                    if kt == 1 and G >= 1:
                        copy_num(G - 1)
                    if g == 0 and c >= 1 and kt in (4, 5):
                        copy_attnT(c - 1, kt - 4)
                    if g == 1 and c >= 1 and kt in (4, 5):
                        copy_x2T(c - 1, kt - 4)
                    if kt == 11 and G + 1 < CHUNKS * GROUPS:
                        copy_max(G + 1)
            copy_num(CHUNKS * GROUPS - 1)
            for k in range(DK):
                copy_attnT(CHUNKS - 1, k)
            for k in range(DK):
                copy_x2T(CHUNKS - 1, k)

            act.wait_ge(gate_centred, 1)
            act.activation(gate_work, gate_work, ACT.Exp).then_inc(gate_exp, 1)
            act.wait_ge(cT_ready, 1)
            act.activation(cT, bank(0, 4)[0:EXPERTS], ACT.Copy).then_inc(cT_copied, 1)
            for c in range(CHUNKS):
                for e in range(FFN):
                    i = FFN * c + e
                    act.wait_ge(h_ready, i + 1)
                    if i >= 2:
                        act.wait_ge(h_read, i - 1)
                    act.activation(tanh_h[:, i % 2, :], bank(2 * (i % 2)), ACT.Tanh, scale=0.5).then_inc(tanh_ready, 1)
                act.wait_ge(act_done, FFN * (c + 1))
                if c >= 1:
                    act.wait_ge(ffnN_ready, 2 * c)
                for d in range(DK):
                    act.activation(ffnT[:, d, :], bank(6 + d), ACT.Copy).then_inc(ffn_copied, 1)

        @block.tensor
        def _(pe):
            pe.wait_ge(ld_wk, 16)
            pe.wait_ge(ld_xT, 16)
            for f in range(SF):
                if f >= 2:
                    pe.wait_ge(k_exp, f - 1)
                for n in range(SEQ // CHUNK):
                    for k in range(DK):
                        mm = pe.matmul(bank(4 * (f % 2) + n), wk_s[:, k, f * P:(f + 1) * P],
                                       xT[:, k, n * CHUNK:(n + 1) * CHUNK], start=(k == 0), stop=(k == DK - 1))
                mm.then_inc(kT_ready, 1)
            pe.wait_ge(ld_wv, 16)
            pe.wait_ge(consts_ready, 1)
            pe.wait_ge(k_exp, 3)
            for t in range(TILES + 1):
                if t < TILES:
                    if t >= 4:
                        pe.wait_ge(v_copied, t - 3)
                    for k in range(DK):
                        mm = pe.matmul(bank(t % 4), xT[:, k, t * P:(t + 1) * P], wv_s[:, k, :],
                                       start=(k == 0), stop=(k == DK - 1))
                    mm.then_inc(v_ready, 1)
                if t >= 1:
                    u = t - 1
                    pe.wait_ge(k_exp, 4)
                    if u >= 2:
                        pe.wait_ge(ek_copied, u - 1)
                    for f in range(SF):
                        mm = pe.transpose(bank(4 + u % 2)[:, f * P:(f + 1) * P], ekT[:, f, u * P:(u + 1) * P],
                                          ident[:, :])
                    mm.then_inc(ekT_ready, 1)
            pe.wait_ge(v_copied, TILES)
            pe.wait_ge(ek_copied, TILES)
            for f in range(SF):
                for t in range(TILES):
                    mm = pe.matmul(bank(6)[:, f * P:(f + 1) * P], v_s[:, t, f * P:(f + 1) * P],
                                   ek[:, t, f * P:(f + 1) * P], start=(t == 0), stop=(t == TILES - 1))
            mm.then_inc(ctx_ready, 1)
            pe.wait_ge(ld_ctx, 16)
            pe.wait_ge(ld_cw, 16 * 3)
            for f in range(DK):
                if f == 1:
                    pe.wait_ge(fold_copied, 1)
                for n in range(0, KEYS, CHUNK):
                    w = min(CHUNK, KEYS - n)
                    for k in range(DK):
                        mm = pe.matmul(bank(4 * f + n // CHUNK)[:, 0:w], wk_c[:, k, f * P:(f + 1) * P],
                                       ctxT[:, k, n:n + w], start=(k == 0), stop=(k == DK - 1))
                mm.then_inc(kc_ready, 1)
                if f == 0:
                    pe.wait_ge(ctx_copied, 2)
                    pe.wait_ge(ld_wo, 16)
                    for j in range(SF):
                        mm = pe.matmul(bank(4 + j // 2)[:, (j % 2) * DIM:(j % 2 + 1) * DIM], context[:, j, :],
                                       wo_s[:, j, :], start=True, stop=True)
                    mm.then_inc(fold_ready, 1)
            pe.wait_ge(ld_wq, 16)
            pe.wait_ge(kc_copied, 2)
            for i in range(TILES + 13):
                if i < TILES:
                    if i >= 2:
                        pe.wait_ge(q_centred, i - 1)
                    for k in range(DK):
                        mm = pe.matmul(bank(i % 2), xT[:, k, i * P:(i + 1) * P], wq_s[:, k, :],
                                       start=(k == 0), stop=(k == DK - 1))
                    mm.then_inc(q_ready, 1)
                t = i - 2
                if 0 <= t < TILES:
                    pe.wait_ge(qn_ready, t + 1)
                    if t >= 2:
                        pe.wait_ge(qT_copied, t - 1)
                    for f in range(SF):
                        mm = pe.transpose(bank(2 + t % 2)[:, f * P:(f + 1) * P],
                                          qnorm[:, t % 2, f * P:(f + 1) * P], ident[:, :])
                    mm.then_inc(qT_ready, 1)
                t = i - 3
                if 0 <= t < TILES:
                    pe.wait_ge(qT_copied, t + 1)
                    if t >= 1:
                        pe.wait_ge(y_read, t)
                    for f in range(SF):
                        mm = pe.matmul(bank(4)[:, 0:DIM], qsT[:, t % 2, f * P:(f + 1) * P], fold[:, f, :],
                                       start=(f == 0), stop=(f == SF - 1))
                    mm.then_inc(y_ready, 1)
                t = i - 6
                if 0 <= t < TILES:
                    pe.wait_ge(x1_ready, t + 1)
                    if t >= 1:
                        pe.wait_ge(x1T_copied, t)
                    for k in range(DK):
                        mm = pe.transpose(bank(5)[:, k * P:(k + 1) * P], x_sb[:, t, k * P:(k + 1) * P], ident[:, :])
                    mm.then_inc(x1T_ready, 1)
                if (i - 10) % TPC == 0 and 0 <= (i - 10) // TPC < CHUNKS:
                    c = (i - 10) // TPC
                    pe.wait_ge(x1T_copied, TPC * (c + 1))
                    if c >= 1:
                        pe.wait_ge(qf_copied, DK * c)
                    for f in range(DK):
                        for k in range(DK):
                            mm = pe.matmul(bank(6 + f), wq_c[:, k, f * P:(f + 1) * P],
                                           xT[:, k, c * CHUNK:(c + 1) * CHUNK], start=(k == 0), stop=(k == DK - 1))
                    mm.then_inc(qp_ready, 1)

            pe.wait_ge(q_centred, TILES)
            pe.wait_ge(qT_copied, TILES)
            for t in range(KT):
                r = krows(t)
                if t >= 4:
                    pe.wait_ge(vc_copied, t - 3)
                for k in range(DK):
                    mm = pe.matmul(bank(t % 4)[0:r, 0:DIM], ctxT[:, k, t * P:t * P + r], wv_c[:, k, :],
                                   start=(k == 0), stop=(k == DK - 1))
                mm.then_inc(vc_ready, 1)

            def max_unit(u):
                G, v = divmod(u, UNITS)
                qt, rest = divmod(v, GROUP * PIECES)
                j, n = divmod(rest, PIECES)
                g = G % GROUPS
                at, w = piece(n)
                if v == 0:
                    pe.wait_ge(q_stacked[g], 16 * SPLIT * (G // GROUPS + 1))
                if u >= len(MAX_BANKS):
                    pe.wait_ge(max_read, u - len(MAX_BANKS) + 1)
                pe.matmul(bank(MAX_BANKS[u % len(MAX_BANKS)])[:, 0:w], qstack[0:SROWS, g, j, qt * P:(qt + 1) * P],
                          kstack[0:SROWS, g * GROUP + j, at:at + w], start=True, stop=True).then_inc(max_scores, 1)

            def turn_max(G):
                pe.wait_ge(max_split, G + 1)
                if G >= 1:
                    pe.wait_ge(maxT_copied, G)
                for t in range(TPC):
                    mm = pe.transpose(bank(5).bitcast(BF16)[0:LEVELS * GROUP, t * P:(t + 1) * P],
                                      mlev[:, t, :, :].rearrange("p k h -> p (k h)"), ident_b[:, :])
                mm.then_inc(maxT_ready, 1)

            def scores(s, j):
                G, kt = divmod(s, KT)
                g, r = G % GROUPS, krows(kt)
                n = GROUP * s + j
                if kt == 0 and j == 0:
                    pe.wait_ge(max_stacked, 16 * LEVELS * (G + 1))
                if n >= ST_BANKS:
                    pe.wait_ge(p_ready, n - ST_BANKS + 1)
                pe.matmul(bank(n % ST_BANKS)[0:r], kstack[0:SROWS + LEVELS, g * GROUP + j, kt * P:kt * P + r],
                          qstack[0:SROWS + LEVELS, g, j, :], start=True, stop=True).then_inc(st_ready, 1)

            def weigh(s):
                G, kt = divmod(s, KT)
                g, r = G % GROUPS, krows(kt)
                pe.wait_ge(p_ready, GROUP * (s + 1))
                if kt == 0 and G >= 1:
                    pe.wait_ge(num_copied, G)
                for j in range(GROUP):
                    mm = pe.matmul(bank(4)[VW * j:VW * (j + 1)], vals[0:r, kt, g * GROUP + j, :],
                                   prob[0:r, s % 3, j, :], start=(kt == 0), stop=(kt == KT - 1))
                mm.then_inc(pv_done, 1)

            def turn_num(G):
                pe.wait_ge(num_copied, G + 1)
                if G + 1 < CHUNKS * GROUPS:
                    pe.wait_ge(maxT_copied, G + 2)
                else:
                    pe.wait_ge(attn_ready, G)
                for t in range(TPC):
                    mm = pe.transpose(bank(5)[:, t * P:(t + 1) * P], numT[:, t * P:(t + 1) * P], ident[:, :])
                mm.then_inc(den_ready, 1)

            def turn_attn(c, k):
                pe.wait_ge(attn_ready, GROUPS * (c + 1))
                if k >= 1:
                    pe.wait_ge(attnT_copied, DK * c + k)
                for t in range(TPC):
                    mm = pe.transpose(bank(5)[:, t * P:(t + 1) * P],
                                      attn[:, t, 2 * k:2 * k + 2, :, :].rearrange("p g h d -> p (g h d)"), ident[:, :])
                mm.then_inc(attnT_ready, 1)

            def out_proj(c, half):
                n = 2 * c + half
                pe.wait_ge(attnT_copied, DK * (c + 1))
                if half == 1:
                    pe.wait_ge(co_read, n)
                if n == 0:
                    pe.wait_ge(ld_woc, 16)
                for q in range(2):
                    t = 2 * half + q
                    for k in range(DK):
                        mm = pe.matmul(bank(5)[:, q * DIM:(q + 1) * DIM], attnT[:, k, t * P:(t + 1) * P],
                                       wo_c[:, k, :], start=(k == 0), stop=(k == DK - 1))
                mm.then_inc(co_ready, 1)

            def turn_x2(c, k):
                pe.wait_ge(x2_ready, TPC * (c + 1))
                if k == 0 and c + 1 < CHUNKS:
                    pe.wait_ge(attn_ready, GROUPS * (c + 1) + 1)
                if k >= 1:
                    pe.wait_ge(x2T_copied, DK * c + k)
                for t in range(TPC):
                    mm = pe.transpose(bank(5)[:, t * P:(t + 1) * P],
                                      x_sb[:, TPC * c + t, k * P:(k + 1) * P], ident[:, :])
                mm.then_inc(x2T_ready, 1)

            pe.wait_ge(qf_copied, DK * CHUNKS)
            pe.wait_ge(vc_copied, KT)
            pe.wait_ge(k_stacked, 16 * SPLIT)
            pe.wait_ge(zeros_ready, 3)
            for u in range(units_until(-1)):
                max_unit(u)
            turn_max(0)
            for s in range(STEPS):
                G, kt = divmod(s, KT)
                c, g = divmod(G, GROUPS)
                units = list(range(units_until(s - 1), units_until(s)))
                for pr in range(2):
                    for u in units[pr:pr + 1]:
                        max_unit(u)
                    scores(s, 2 * pr)
                    scores(s, 2 * pr + 1)
                for u in units[2:3]:
                    max_unit(u)
                if s >= 1:
                    weigh(s - 1)
                for u in units[3:]:
                    max_unit(u)
                if kt == 2 and G >= 1:
                    turn_num(G - 1)
                if g == 0 and c >= 1:
                    if kt in (4, 5):
                        turn_attn(c - 1, kt - 4)
                    if kt in (6, 7):
                        out_proj(c - 1, kt - 6)
                if g == 1 and c >= 1 and kt in (4, 5):
                    turn_x2(c - 1, kt - 4)
                if kt == 10 and G + 1 < CHUNKS * GROUPS:
                    if g == 0 and c >= 1:
                        pe.wait_ge(co_read, 2 * c)
                    elif g == 1 and c >= 1:
                        pe.wait_ge(x2T_copied, DK * c)
                    elif G >= 1:
                        pe.wait_ge(attn_ready, G)
                    turn_max(G + 1)
            weigh(STEPS - 1)
            turn_num(CHUNKS * GROUPS - 1)
            for k in range(DK):
                turn_attn(CHUNKS - 1, k)
            for half in range(2):
                out_proj(CHUNKS - 1, half)
            for k in range(DK):
                turn_x2(CHUNKS - 1, k)

            pe.wait_ge(x2T_copied, DK * CHUNKS)
            pe.wait_ge(ld_bias, 16 * 7)
            for t in range(TILES):
                for k in range(DK):
                    mm = pe.matmul(bank(5)[:, t * EXPERTS:(t + 1) * EXPERTS], xT[:, k, t * P:(t + 1) * P],
                                   gate_wT[:, k, :], start=(k == 0), stop=(k == DK - 1))
            mm.then_inc(logits_ready, 1)
            pe.wait_ge(combine_ready, 1)
            for t in range(TILES):
                mm = pe.transpose(psum[0:EXPERTS, t * P:(t + 1) * P], probs[:, t, :], ident[:, :])
            mm.then_inc(cT_ready, 1)
            pe.wait_ge(cT_copied, 1)
            pe.wait_ge(sel_ready, 1)
            pe.wait_ge(ld_w1, 16 * 8)
            pe.wait_ge(ld_w2, 32)

            def hidden(i):
                c, e = divmod(i, FFN)
                if i >= 2:
                    pe.wait_ge(h_read, i - 1)
                for b, w in enumerate((w1T, w3T)):
                    for k in range(DK):
                        mm = pe.matmul(bank(2 * (i % 2) + b), w[:, k, e, :], xT[:, k, c * CHUNK:(c + 1) * CHUNK],
                                       start=(k == 0), stop=(k == DK - 1))
                mm.then_inc(h_ready, 1)
                if e < EXPERTS:
                    if i >= 1:
                        pe.wait_ge(gated, EXPERTS * c + e)
                    pe.matmul(bank(4), expert_sel[:, e, :], cT[:, c * CHUNK:(c + 1) * CHUNK],
                              start=True, stop=True).then_inc(cb_ready, 1)

            def second(i):
                c, e = divmod(i, FFN)
                if e < EXPERTS:
                    pe.wait_ge(gated, EXPERTS * c + e + 1)
                else:
                    pe.wait_ge(h_read, i + 1)
                if e == 0 and c >= 1:
                    pe.wait_ge(ffn_copied, DK * c)
                for d in range(DK):
                    mm = pe.matmul(bank(6 + d), w2T[:, e, d * P:(d + 1) * P], act_h[:, i % 2, :],
                                   start=(e == 0), stop=(e == FFN - 1))
                mm.then_inc(act_done, 1)

            def turn_ffn(c, half):
                n = 2 * c + half
                pe.wait_ge(ffn_copied, DK * (c + 1))
                if n >= 1:
                    pe.wait_ge(ffnN_read, n)
                for q in range(2):
                    t = 2 * half + q
                    for d in range(DK):
                        mm = pe.transpose(bank(5)[:, q * DIM + d * P:q * DIM + (d + 1) * P],
                                          ffnT[:, d, t * P:(t + 1) * P], ident[:, :])
                mm.then_inc(ffnN_ready, 1)

            for i in range(CHUNKS * FFN + 1):
                c, e = divmod(i, FFN)
                if i < CHUNKS * FFN:
                    hidden(i)
                if i >= 1:
                    second(i - 1)
                if c >= 1 and c < CHUNKS and e in (2, 4):
                    turn_ffn(c - 1, e // 2 - 1)
            for half in range(2):
                turn_ffn(CHUNKS - 1, half)

        @block.vector
        def _(dve):
            n = [0]

            def link(ins):
                n[0] += 1
                ins.then_inc(vec_step, 1)
                dve.wait_ge(vec_step, n[0])

            for f in range(SF):
                dve.wait_ge(kT_ready, f + 1)
                dve.tensor_reduce(nkmax[:, f:f + 1], bank(4 * (f % 2), 4), X, ALU.max, negate=True).then_inc(kmax_ready, 1)
            for t in range(TILES):
                dve.wait_ge(v_ready, t + 1)
                dve.tensor_copy(v_s[:, t, :], bank(t % 4)).then_inc(v_copied, 1)
            dve.wait_ge(k_exp, SF)
            link(dve.reciprocal(krec[:, :], ksum[:, :]))
            dve.wait_ge(ctx_ready, 1)
            dve.wait_ge(zeros_ready, 1)
            for half in (0, S_DH):
                dve.tensor_copy(context[half:half + S_DH, :, half:half + S_DH],
                                bank(6)[half:half + S_DH, :].rearrange("p (f n) -> p f n", f=SF)
                                [:, :, half:half + S_DH]).then_inc(ctx_copied, 1)
            dve.wait_ge(fold_ready, 1)
            for j in range(SF):
                ins = dve.tensor_scalar(fold[:, j, :], bank(4 + j // 2)[:, (j % 2) * DIM:(j % 2 + 1) * DIM],
                                        krec[:, j:j + 1], S_SCALE, ALU.mult, ALU.mult)
            ins.then_inc(fold_copied, 1)
            for f in range(DK):
                dve.wait_ge(kc_copied, f + 1)
                link(dve.tensor_scalar(kf[:, f, :], kf[:, f, :], C_SCALE, None, ALU.mult))
                link(dve.tensor_copy(kpart[:, 0, f, :], kf[:, f, :]))
                link(dve.tensor_tensor(kres, kf[:, f, :], kpart[:, 0, f, :], ALU.subtract))
                link(dve.tensor_copy(kpart[:, 1, f, :], kres))
                link(dve.tensor_tensor(kres, kres, kpart[:, 1, f, :], ALU.subtract))
                ins = dve.tensor_copy(kpart[:, 2, f, :], kres)
                if f == DK - 1:
                    ins.then_inc(k_split, 1)
                else:
                    link(ins)
            dve.wait_ge(k_written, 16 * LEVELS)

            def norm_stats(r, at, last, signal):
                link(dve.bn_stats(stats[:, at, :], r))
                link(dve.bn_aggr(meanvar[:, at, :], stats[:, at, :]))

            qmax = [small[:, 32 * b:32 * b + S_HEADS] for b in range(2)]
            qsum = [small[:, 32 * b + 8:32 * b + 8 + S_HEADS] for b in range(2)]
            qrec = [small[:, 32 * b + 16:32 * b + 16 + S_HEADS] for b in range(2)]

            def heads(ap):
                return ap.rearrange("p (h d) -> p h d", h=S_HEADS)

            def spread(ap):
                return ap.rearrange("p (h o) -> p h o", o=1).broadcast_to([P, S_HEADS, S_DH])

            for i in range(TILES + 13):
                t = i - 4
                if 0 <= t < TILES:
                    dve.wait_ge(y_ready, t + 1)
                    dve.wait_ge(x_biased, t + 1)
                    if t >= 2:
                        dve.wait_ge(x1_ready, t - 1)
                    dve.tensor_tensor(resid[:, t % 2, :], bank(4)[:, 0:DIM], x_sb[:, t, :], ALU.add).then_inc(y_read, 1)
                    dve.wait_ge(y_read, t + 1)
                    norm_stats(resid[:, t % 2, :], t % TPC, None, None)
                    dve.tensor_scalar(var_eps[:, t % TPC:t % TPC + 1], meanvar[:, t % TPC, 1:2], EPS, None,
                                      ALU.add).then_inc(b_var, 1)
                t = i - 5
                if 0 <= t < TILES:
                    dve.wait_ge(b_rstd, t + 1)
                    dve.tensor_scalar(x_sb[:, t, :], resid[:, t % 2, :], meanvar[:, t % TPC, 0:1],
                                      rstd[:, t % TPC:t % TPC + 1], ALU.subtract, ALU.mult).then_inc(x1_ready, 1)
                if i < TILES:
                    dve.wait_ge(q_ready, i + 1)
                    if i >= 2:
                        dve.wait_ge(q_centred, i - 1)
                        dve.wait_ge(qn_ready, i - 1)
                    link(dve.tensor_reduce(qmax[i % 2], heads(bank(i % 2)), X, ALU.max))
                    dve.tensor_tensor(heads(qexp[:, i % 2, :]), heads(bank(i % 2)), spread(qmax[i % 2]),
                                      ALU.subtract).then_inc(q_centred, 1)
                t = i - 1
                if 0 <= t < TILES:
                    dve.wait_ge(q_exp, t + 1)
                    link(dve.tensor_reduce(qsum[t % 2], heads(qexp[:, t % 2, :]), X, ALU.add))
                    link(dve.reciprocal(qrec[t % 2], qsum[t % 2]))
                    if t >= 2:
                        dve.wait_ge(qT_ready, t - 1)
                    dve.tensor_tensor(heads(qnorm[:, t % 2, :]), heads(qexp[:, t % 2, :]), spread(qrec[t % 2]),
                                      ALU.mult).then_inc(qn_ready, 1)
                if (i - 12) % TPC == 0 and 0 <= (i - 12) // TPC < CHUNKS:
                    c = (i - 12) // TPC
                    dve.wait_ge(qf_copied, DK * (c + 1))
                    if c >= 1:
                        dve.wait_ge(q_written, 16 * c)
                    link(dve.tensor_copy(qpart[:, 0, :], qf))
                    link(dve.tensor_tensor(qres, qf, qpart[:, 0, :], ALU.subtract))
                    link(dve.tensor_copy(qpart[:, 1, :], qres))
                    link(dve.tensor_tensor(qres, qres, qpart[:, 1, :], ALU.subtract))
                    dve.tensor_copy(qpart[:, 2, :], qres).then_inc(q_split, 1)

            dve.wait_ge(zeros_ready, 3)
            dve.wait_ge(ld_bias, 16 * 7)
            for t in range(KT):
                r = krows(t)
                dve.wait_ge(vc_ready, t + 1)
                dve.tensor_tensor(vals[0:r, t, :, 0:C_DH],
                                  bank(t % 4)[0:r, 0:DIM].rearrange("p (h d) -> p h d", h=C_HEADS),
                                  bv_row[0:r, :].rearrange("p (h d) -> p h d", h=C_HEADS),
                                  ALU.add).then_inc(vc_copied, 1)

            def read_max(u):
                w = piece(u % PIECES)[1]
                dve.wait_ge(max_scores, u + 1)
                v = u % UNITS
                dve.tensor_reduce(mpart[:, u // UNITS % 2, v // PIECES, v % PIECES:v % PIECES + 1], bank(MAX_BANKS[u % len(MAX_BANKS)])[:, 0:w], X,
                                  ALU.max).then_inc(max_read, 1)

            def split_max(G, n):
                lev = [mlev[:, :, k, :] for k in range(LEVELS)]
                neg = negmax[:, :].rearrange("p (t h) -> p t h", t=TPC)
                res = nres[:, :].rearrange("p (t h) -> p t h", t=TPC)
                if n == 0:
                    dve.wait_ge(max_read, UNITS * (G + 1))
                    ins = dve.tensor_reduce(negmax[:, :], mpart[:, G % 2, :, :], X, ALU.max, negate=True)
                elif n == 1:
                    if G >= 1:
                        dve.wait_ge(maxT_ready, G)
                    ins = dve.tensor_copy(lev[0], neg)
                elif n == 2:
                    ins = dve.tensor_tensor(res, neg, lev[0], ALU.subtract)
                elif n == 3:
                    ins = dve.tensor_copy(lev[1], res)
                elif n == 4:
                    ins = dve.tensor_tensor(res, res, lev[1], ALU.subtract)
                else:
                    dve.tensor_copy(lev[2], res).then_inc(max_split, 1)
                if n < SPLIT_STEPS - 1:
                    link(ins)

            def divide(G):
                dve.wait_ge(den_ready, G + 1)
                num = bank(5).rearrange("p (t h w) -> p t h w", t=TPC, h=GROUP)
                link(dve.reciprocal(den_rec[:, :, :, :], num[:, :, :, C_DH:C_DH + 1]))
                if G >= GROUPS:
                    dve.wait_ge(attnT_ready, DK * (G // GROUPS))
                dve.tensor_tensor(attn[:, :, G % GROUPS, :, :], num[:, :, :, 0:C_DH],
                                  den_rec[:, :, :, :].broadcast_to([P, TPC, GROUP, C_DH]),
                                  ALU.mult).then_inc(attn_ready, 1)

            def add_residual(c, half, ready, read):
                k = 2 * c + half
                dve.wait_ge(ready, k + 1)
                at = TPC * c + 2 * half
                dve.tensor_tensor(x_sb[:, at:at + 2, :], bank(5).rearrange("p (t n) -> p t n", t=2),
                                  x_sb[:, at:at + 2, :], ALU.add).then_inc(read, 1)
                dve.wait_ge(read, k + 1)
                for q in range(2):
                    norm_stats(x_sb[:, at + q, :], 2 * half + q, None, None)

            def normalise(c, rsig, done):
                dve.wait_ge(rsig, c + 1)
                for t in range(TPC):
                    dve.tensor_scalar(x_sb[:, TPC * c + t, :], x_sb[:, TPC * c + t, :], meanvar[:, t, 0:1],
                                      rstd[:, t:t + 1], ALU.subtract, ALU.mult).then_inc(done, 1)

            def add_eps(sig):
                dve.tensor_scalar(var_eps[:, :], meanvar[:, :, 1], EPS, None, ALU.add).then_inc(sig, 1)

            def reads(lo, hi):
                for u in range(lo, hi):
                    read_max(u)
                    if u >= UNITS and u % UNITS < SPLIT_STEPS:
                        split_max(u // UNITS - 1, u % UNITS)
                    if u == CHUNKS * GROUPS * UNITS - 1:
                        for step in range(SPLIT_STEPS):
                            split_max(u // UNITS, step)

            dve.wait_ge(x1_biased, TILES)
            reads(0, units_until(-1))
            for s in range(STEPS):
                G, kt = divmod(s, KT)
                c, g = divmod(G, GROUPS)
                reads(units_until(s - 1), units_until(s))
                if kt == 3 and G >= 1:
                    divide(G - 1)
                if g == 0 and c >= 1:
                    if kt in (7, 8):
                        add_residual(c - 1, kt - 7, co_ready, co_read)
                    if kt == 8:
                        add_eps(c_var)
                    if kt == 9:
                        normalise(c - 1, c_rstd, x2_ready)
            divide(CHUNKS * GROUPS - 1)
            for half in range(2):
                add_residual(CHUNKS - 1, half, co_ready, co_read)
            add_eps(c_var)
            normalise(CHUNKS - 1, c_rstd, x2_ready)

            def flat(ap):
                return ap.rearrange("p t e -> p (t e)")

            def wide(ap):
                return ap.rearrange("p (t o) -> p t o", o=1).broadcast_to([P, TILES, EXPERTS])

            logit = bank(5)[:, 0:TILES * EXPERTS].rearrange("p (t e) -> p t e", t=TILES)
            work, equal, count = gate_work, gate_equal, gate_count
            one, two = small[:, 0:TILES], small[:, 16:16 + TILES]
            dve.wait_ge(logits_ready, 1)
            dve.wait_ge(sel_ready, 1)
            link(dve.tensor_reduce(one, logit, X, ALU.max))
            dve.tensor_tensor(work, logit, wide(one), ALU.subtract).then_inc(gate_centred, 1)
            dve.wait_ge(gate_exp, 1)
            link(dve.tensor_reduce(one, work, X, ALU.add))
            link(dve.reciprocal(one, one))
            link(dve.tensor_tensor(probs, work, wide(one), ALU.mult))
            for t in range(TILES):
                ins = dve.max(top8[:, t, :], probs[:, t, :])
            link(ins)
            fourth = top8[:, :, TOPK - 1:TOPK].broadcast_to([P, TILES, EXPERTS])
            link(dve.tensor_tensor(equal, probs, fourth, ALU.is_equal))
            link(dve.tensor_tensor(work, probs, fourth, ALU.is_gt))
            link(dve.tensor_reduce(one, work, X, ALU.add))
            link(dve.tensor_scalar(one, one, -1.0, float(TOPK), ALU.mult, ALU.add))
            link(dve.tensor_tensor_scan(flat(count), flat(equal), flat(zero_gate), 0.0, ALU.add, ALU.add))
            link(dve.tensor_tensor(two[:, 1:TILES], one[:, 1:TILES], count[:, 0:TILES - 1, EXPERTS - 1], ALU.add))
            link(dve.tensor_copy(two[:, 0:1], one[:, 0:1]))
            link(dve.tensor_tensor(count, count, wide(two), ALU.is_le))
            link(dve.tensor_tensor(equal, equal, count, ALU.mult))
            link(dve.tensor_tensor(work, work, equal, ALU.add))
            link(dve.tensor_tensor(probs, probs, work, ALU.mult))
            link(dve.tensor_reduce(one, probs, X, ALU.add))
            link(dve.reciprocal(one, one))
            dve.tensor_tensor(probs, probs, wide(one), ALU.mult).then_inc(combine_ready, 1)

            for c in range(CHUNKS):
                for e in range(FFN):
                    i = FFN * c + e
                    b = 2 * (i % 2)
                    dve.wait_ge(tanh_ready, i + 1)
                    link(dve.scalar_tensor_tensor(out=silu_h, in0=tanh_h[:, i % 2, :], scalar=1.0, in1=bank(b),
                                                  op0=ALU.add, op1=ALU.mult))
                    dst = hprod if e < EXPERTS else act_h[:, i % 2, :]
                    if e == EXPERTS and i >= 2:
                        dve.wait_ge(act_done, i - 1)
                    dve.scalar_tensor_tensor(out=dst, in0=silu_h, scalar=0.5, in1=bank(b + 1),
                                             op0=ALU.mult, op1=ALU.mult).then_inc(h_read, 1)
                    dve.wait_ge(h_read, i + 1)
                    if e < EXPERTS:
                        dve.wait_ge(cb_ready, EXPERTS * c + e + 1)
                        if i >= 2:
                            dve.wait_ge(act_done, i - 1)
                        dve.tensor_tensor(act_h[:, i % 2, :], hprod, bank(4), ALU.mult).then_inc(gated, 1)
                    if c >= 1 and e in (3, 5):
                        add_residual(c - 1, e // 2 - 1, ffnN_ready, ffnN_read)
                    if c >= 1 and e == 5:
                        add_eps(d_var)
                    if c >= 1 and e == 6:
                        normalise(c - 1, d_rstd, out_ready)
            for half in range(2):
                add_residual(CHUNKS - 1, half, ffnN_ready, ffnN_read)
            add_eps(d_var)
            normalise(CHUNKS - 1, d_rstd, out_ready)


def _launch_arrays(i):
    import numpy as np

    def arr(x):
        return np.ascontiguousarray(x)

    n = {k: np.asarray(v) for k, v in i.items()}
    out = {
        "x": arr(n["x"][0]), "xT": arr(n["x"][0].T), "ctxT": arr(n["ctx_1024"][0].T),
        "bq2": arr(n["L0_xattn_bq"].reshape(DK, P).T), "bk2": arr(n["L0_xattn_bk"].reshape(DK, P).T),
        "gateT": arr(n["L0_ffn_gate_w"].T),
        "w1T": arr(n["L0_ffn_w1"].transpose(2, 0, 1)), "w3T": arr(n["L0_ffn_w3"].transpose(2, 0, 1)),
        "w2T": arr(n["L0_ffn_w2"].transpose(2, 0, 1)),
        "sw1T": arr(n["L0_ffn_sw1"].T), "sw3T": arr(n["L0_ffn_sw3"].T), "sw2T": arr(n["L0_ffn_sw2"].T),
    }
    for k in ("L0_attn_Wq", "L0_attn_Wk", "L0_attn_Wv", "L0_attn_Wo", "L0_attn_bo", "L0_xattn_Wq",
              "L0_xattn_Wk", "L0_xattn_Wv", "L0_xattn_bv", "L0_xattn_Wo", "L0_xattn_bo"):
        out[k] = arr(n[k])
    return out


def kernel(**inputs):
    import numpy as np
    import concourse.bacc as bacc
    from concourse.bass_utils import run_bass_kernel_spmd

    nc = bacc.Bacc("TRN2", target_bir_lowering=False, num_devices=1)
    given = _launch_arrays(inputs)
    arrays = {f"in_{k}": v for k, v in given.items()}
    aps = {k: nc.dram_tensor(f"in_{k}", v.shape, mybir.dt.from_np(v.dtype), kind="ExternalInput").ap()
           for k, v in given.items()}
    out = nc.dram_tensor("out_dram", (SEQ, DIM), F32, kind="ExternalOutput").ap()
    decoder_layer(nc, aps, out)
    got = run_bass_kernel_spmd(nc, [arrays], core_ids=[0]).results[0]["out_dram"]
    return np.asarray(got).reshape(1, SEQ, DIM)
```

```python
from contextlib import ExitStack

import concourse.bass as bass
from concourse import mybir

F32 = mybir.dt.float32
BF16 = mybir.dt.bfloat16
F32R = mybir.dt.float32r
ALU = mybir.AluOpType
ACT = mybir.ActivationFunctionType
X = mybir.AxisListType.X

P = 128
SEQ, DIM = 2048, 256
KEYS = 1601
TILES = SEQ // P
CHUNK = 512
CHUNKS = SEQ // CHUNK
TPC = CHUNK // P
DK = DIM // P
S_HEADS, S_DH = 8, 64
S_HID = S_HEADS * S_DH
SF = S_HID // P
S_SCALE = S_DH ** -0.5
C_HEADS, C_DH = 16, 16
C_SCALE = C_DH ** -0.5
GROUP = 4
GROUPS = C_HEADS // GROUP
KT = -(-KEYS // P)
LASTK = KEYS - (KT - 1) * P
VW = P // GROUP
SPLIT = 6
LEVELS = 3
SROWS = SPLIT * C_DH
Q_LEVEL = (0, 0, 0, 1, 1, 2)
K_LEVEL = (0, 1, 2, 0, 1, 0)
PIECES = 4
PW = -(-KEYS // PIECES)
UNITS = TPC * GROUP * PIECES
SPLIT_STEPS = 6
LEAD = KT + 3
EXPERTS, HID, TOPK = 16, 128, 4
FFN = EXPERTS + 1
EW = 2 * DK * HID + DIM
W_SLOTS = 4
AHEAD = 3
GATE_FIRST = (CHUNKS - 1) * TPC
EPS = 1e-5


R3 = -(-(5 * 1024 + DK * KEYS + 3 * DK * DIM) // 8) * 8


def krows(kt):
    return P if kt < KT - 1 else LASTK


def buffer(G):
    return (G + 1) % GROUPS


def piece(n):
    at = 0 if n == 0 else PW + (n - 1) * (PW - 1)
    return at, PW if n == 0 else PW - 1


assert sum(piece(n)[1] for n in range(PIECES)) == KEYS and LASTK > 0


def decoder_layer(nc, a, out):
    with ExitStack() as ctx:
        def sb(name, shape, dt=F32):
            return ctx.enter_context(nc.sbuf_tensor(name, shape, dt))

        def sem(name):
            return ctx.enter_context(nc.semaphore(name))

        kparts_d = nc.dram_tensor("kparts_d", (LEVELS, DIM, KEYS), BF16).ap()
        qparts_d = nc.dram_tensor("qparts_d", (LEVELS, DIM, SEQ), BF16).ap()

        psum = ctx.enter_context(nc.psum_tensor("psum", [P, 8 * CHUNK], F32))

        def bank(n, w=1):
            return psum[:, n * CHUNK:(n + w) * CHUNK]

        MAX_BANKS = (3, 6, 7)
        ST_BANKS = 3

        x_sb = sb("x_sb", [P, TILES, DIM])
        numT = sb("numT", [P, CHUNK])
        attn = sb("attn", [P, TPC, GROUPS, GROUP, C_DH])
        attnT = sb("attnT", [P, DK, CHUNK])
        wo_c = sb("wo_c", [P, DK, DIM])
        den_rec = sb("den_rec", [P, TPC, GROUP, 1])
        ident = sb("ident", [P, P])
        ident_b = sb("ident_b", [P, P], BF16)
        half_neg = sb("half_neg", [P, TPC])
        stats = sb("stats", [P, TPC, 6])
        meanvar = sb("meanvar", [P, TPC, 2])
        var_eps = sb("var_eps", [P, TPC])
        rstd = sb("rstd", [P, TPC])
        bq_c = sb("bq_c", [P, DK])
        bk_c = sb("bk_c", [P, DK])
        small = sb("small", [P, 64])
        mpart = sb("mpart", [P, 2, TPC * GROUP, PIECES])
        negmax = sb("negmax", [P, TPC * GROUP])
        nres = sb("nres", [P, TPC * GROUP])
        mlev = sb("mlev", [P, TPC, LEVELS, GROUP], BF16)
        maxT = sb("maxT", [LEVELS * GROUP, 2, CHUNK], BF16)

        bo_row = sb("bo_row", [P, DIM])
        bv_row = sb("bv_row", [P, DIM])
        boc_row = sb("boc_row", [P, DIM])
        nkmax = sb("nkmax", [P, SF])
        ksum = sb("ksum", [P, SF])
        krec = sb("krec", [P, SF])
        gate_wT = sb("gate_wT", [P, DK, EXPERTS])
        logits, probs, zero_gate, gate_work, gate_equal, gate_count = (
            sb(name, [P, TILES, EXPERTS]) for name in
            ("logits", "probs", "zero_gate", "gate_work", "gate_equal", "gate_count"))
        top8 = sb("top8", [P, TILES, 8])
        gate_parts = sb("gate_parts", [P, TILES, 2, EXPERTS], F32R)
        sel_f = sb("sel_f", [P, EXPERTS])
        expert_sel = sb("expert_sel", [P, EXPERTS], F32R)
        tanh_h = sb("tanh_h", [P, 2, CHUNK])
        weighted = sb("weighted", [P, CHUNK])
        ffnT = attnT

        in_attention = ExitStack()

        def early(name, shape):
            return in_attention.enter_context(nc.sbuf_tensor(name, shape, F32))

        xT = early("xT", [P, DK, SEQ])
        region3 = early("region3", [P, R3])

        region1 = early("region1", [P, C_HEADS * (KEYS + 1) // 2 + KT * C_HEADS * VW])
        ekT = region1[:, 0:SF * SEQ].rearrange("p (f n) -> p f n", f=SF)
        v_s = region1[:, SF * SEQ:2 * SF * SEQ].rearrange("p (t n) -> p t n", t=TILES)
        KW = C_HEADS * KEYS // 2
        kstack = region1[:, 0:KW].bitcast(BF16).rearrange("p (h n) -> p h n", h=C_HEADS)
        vals = region1[:, KW:KW + KT * C_HEADS * VW].rearrange("p (t h w) -> p t h w", t=KT, h=C_HEADS)

        region2 = early("region2", [P, 4 * CHUNK // 2 * GROUP + 3 * GROUP * CHUNK])

        def r2(at, n):
            return region2[:, at:at + n]

        ek = r2(0, TILES * CHUNK).rearrange("p (t n) -> p t n", t=TILES)
        context = r2(TILES * CHUNK, SF * P).rearrange("p (f n) -> p f n", f=SF)
        kf = r2(0, DK * KEYS).rearrange("p (f n) -> p f n", f=DK)
        kres = r2(DK * KEYS, KEYS)
        kpart = r2(3 * KEYS + 1, 3 * KEYS + 3).bitcast(BF16)[:, 0:DK * LEVELS * KEYS].rearrange(
            "p (k f n) -> p k f n", k=LEVELS, f=DK)
        qexp = r2(0, 2 * S_HID).rearrange("p (b n) -> p b n", b=2)
        qnorm = r2(1024, 2 * S_HID).rearrange("p (b n) -> p b n", b=2)
        qsT = r2(2048, 2 * S_HID).rearrange("p (b n) -> p b n", b=2)
        resid = r2(3072, 2 * DIM).rearrange("p (b n) -> p b n", b=2)
        qf = r2(3584, DK * CHUNK)
        qres = r2(4608, DK * CHUNK)
        qpart = r2(5632, LEVELS * DK * CHUNK // 2).bitcast(BF16).rearrange("p (k n) -> p k n", k=LEVELS)
        qstack = r2(3 * GROUP * CHUNK, 4 * GROUP * CHUNK // 2).bitcast(BF16).rearrange("p (b h n) -> p b h n", b=4, h=GROUP)
        prob = r2(0, 3 * GROUP * CHUNK).rearrange("p (b h n) -> p b h n", b=3, h=GROUP)

        def r3(at, n, **k):
            return region3[:, at:at + n]

        wq_s, wk_s, wv_s = (r3(1024 * n, 1024).rearrange("p (k n) -> p k n", k=DK) for n in range(3))
        wo_s = r3(3072, 1024).rearrange("p (f n) -> p f n", f=SF)
        fold = r3(4096, 1024).rearrange("p (f n) -> p f n", f=SF)
        ctxT = r3(5120, DK * KEYS).rearrange("p (k n) -> p k n", k=DK)
        wq_c, wk_c, wv_c = (r3(5120 + DK * KEYS + 512 * n, 512).rearrange("p (k n) -> p k n", k=DK)
                            for n in range(3))


        in_attention.close()
        x2_hi = sb("x2_hi", [P, DK, SEQ], F32R)
        x2_lo = sb("x2_lo", [P, DK, SEQ], F32R)
        comb = sb("comb", [P, SEQ], F32R)
        w_raw = sb("w_raw", [P, W_SLOTS, EW])
        blend_s = sb("blend_s", [P, CHUNK])
        sb("rest_of_region3", [P, R3 - DK * SEQ - SEQ - W_SLOTS * EW - CHUNK])
        w_hi = sb("w_hi", [P, FFN, EW], F32R)
        w_lo = sb("w_lo", [P, FFN, EW], F32R)
        act_hi = sb("act_hi", [P, 2, CHUNK], F32R)
        act_lo = sb("act_lo", [P, 2, CHUNK], F32R)
        act_h = sb("act_h", [P, 2, CHUNK])
        silu_h = sb("silu_h", [P, CHUNK])

        def sems(*names):
            return [sem(n) for n in names]

        ld_xT, ld_wk, ld_wv, ld_wq, ld_wo, ld_x, ld_ctx, ld_cw, ld_bias, ld_woc = sems(
            "ld_xT", "ld_wk", "ld_wv", "ld_wq", "ld_wo", "ld_x", "ld_ctx", "ld_cw", "ld_bias", "ld_woc")
        (consts_ready, zeros_ready, x_biased, kT_ready, kmax_ready, k_exp, v_ready, v_copied, ekT_ready,
         ek_copied, ctx_ready, ctx_copied, fold_ready, fold_copied) = sems(
            "consts_ready", "zeros_ready", "x_biased", "kT_ready", "kmax_ready", "k_exp", "v_ready",
            "v_copied", "ekT_ready", "ek_copied", "ctx_ready", "ctx_copied", "fold_ready", "fold_copied")
        kc_ready, kc_copied, k_split, k_written, k_stacked, vc_ready, vc_copied = sems(
            "kc_ready", "kc_copied", "k_split", "k_written", "k_stacked", "vc_ready", "vc_copied")
        (q_ready, q_centred, q_exp, qn_ready, qT_ready, qT_copied, y_ready, y_read, b_var, b_rstd,
         x1_ready, x1T_ready, x1T_copied, qp_ready, qf_copied, q_split, q_written) = sems(
            "q_ready", "q_centred", "q_exp", "qn_ready", "qT_ready", "qT_copied", "y_ready", "y_read",
            "b_var", "b_rstd", "x1_ready", "x1T_ready", "x1T_copied", "qp_ready", "qf_copied", "q_split",
            "q_written")
        q_stacked = sems(*(f"q_stacked{g}" for g in range(GROUPS)))
        (max_scores, max_read, max_split, maxT_ready, maxT_copied, max_stacked, st_ready, p_ready,
         pv_done, num_copied, den_ready, attn_ready, co_ready, co_read, c_var, c_rstd, x2_ready, x2T_ready,
         x2T_copied) = sems(
            "max_scores", "max_read", "max_split", "maxT_ready", "maxT_copied", "max_stacked",
            "st_ready", "p_ready", "pv_done", "num_copied", "den_ready", "attn_ready", "co_ready", "co_read",
            "c_var", "c_rstd", "x2_ready", "x2T_ready", "x2T_copied")
        gate_centred, gate_exp, zero_ready = sems("gate_centred", "gate_exp", "zero_ready")
        ld_w = sems(*(f"ld_w{n}" for n in range(W_SLOTS)))
        w_hi_ready, w_lo_ready, x2_hi_ready, x2_lo_ready, logits_copied, comb_copied, gate_turned, gate_ready = sems(
            "w_hi_ready", "w_lo_ready", "x2_hi_ready", "x2_lo_ready", "logits_copied", "comb_copied",
            "gate_turned", "gate_ready")
        blend_ready, blend_copied, weighted_ready, act_ready, act_hi_ready, act_lo_ready = sems(
            "blend_ready", "blend_copied", "weighted_ready", "act_ready", "act_hi_ready", "act_lo_ready")
        sel_ready, x1_biased, attnT_ready, attnT_copied = sems("sel_ready", "x1_biased", "attnT_ready", "attnT_copied")
        (logits_ready, h_ready, tanh_ready, h_read,
         act_done, ffn_copied, ffnN_ready, ffnN_read, d_var, d_rstd, out_ready, out_written) = sems(
            "logits_ready", "h_ready", "tanh_ready",
            "h_read", "act_done", "ffn_copied", "ffnN_ready", "ffnN_read",
            "d_var", "d_rstd", "out_ready", "out_written")
        vec_step = sem("vec_step")
        pool_step = sem("pool_step")

        block = ctx.enter_context(nc.Block())

        def units_until(step):
            return min(CHUNKS * GROUPS * UNITS, -(-UNITS * (step + 1 + LEAD) // KT))

        STEPS = CHUNKS * GROUPS * KT

        @block.sync
        def _(sp):
            sp.dma_start(xT[:, :, :], a["xT"].rearrange("(k p) n -> p k n", p=P)).then_inc(ld_xT, 16)
            sp.dma_start(wv_s, a["L0_attn_Wv"].rearrange("(k p) n -> p k n", p=P)).then_inc(ld_wv, 16)
            sp.dma_start(ctxT, a["ctxT"].rearrange("(k p) n -> p k n", p=P)).then_inc(ld_ctx, 16)
            sp.dma_start(wq_s, a["L0_attn_Wq"].rearrange("(k p) n -> p k n", p=P)).then_inc(ld_wq, 16)
            for w, name in ((wq_c, "L0_xattn_Wq"), (wk_c, "L0_xattn_Wk"), (wv_c, "L0_xattn_Wv")):
                sp.dma_start(w, a[name].rearrange("(k p) n -> p k n", p=P)).then_inc(ld_cw, 16)
            sp.dma_start(wo_c[:, :, :], a["L0_xattn_Wo"].rearrange("(k p) n -> p k n", p=P)).then_inc(ld_woc, 16)
            sp.wait_ge(k_split, 1)
            for k in range(LEVELS):
                sp.dma_start(kparts_d[k].rearrange("(f p) n -> p f n", p=P), kpart[:, k]).then_inc(k_written, 16)
            sp.wait_ge(k_written, 16 * LEVELS)
            for b in range(SPLIT):
                sp.dma_start(kstack[C_DH * b:C_DH * b + C_DH, :, :],
                             kparts_d[K_LEVEL[b]].rearrange("(h d) n -> d h n", d=C_DH)).then_inc(k_stacked, 16)
            def load_weights(e):
                slot = e % W_SLOTS
                if e >= W_SLOTS:
                    sp.wait_ge(w_lo_ready, e - W_SLOTS + 1)
                for n, name in enumerate(("w1T", "w3T")):
                    src = a[name][:, e, :] if e < EXPERTS else a["s" + name]
                    sp.dma_start(w_raw[:, slot, n * DK * HID:(n + 1) * DK * HID].rearrange("p (k n) -> p k n", k=DK),
                                 src.rearrange("(k p) n -> p k n", p=P)).then_inc(ld_w[slot], 16)
                sp.dma_start(w_raw[:, slot, 2 * DK * HID:EW],
                             a["w2T"][:, e, :] if e < EXPERTS else a["sw2T"]).then_inc(ld_w[slot], 16)

            def stack_queries(G):
                c, g = divmod(G, GROUPS)
                if G == GROUPS - 1:
                    sp.wait_ge(q_written, 16 * CHUNKS)
                if G >= 4:
                    sp.wait_ge(st_ready, GROUP * KT * (G - 3))
                for b in range(SPLIT):
                    sp.dma_start(
                        qstack[C_DH * b:C_DH * b + C_DH, buffer(G), :, :],
                        qparts_d[Q_LEVEL[b], g * GROUP * C_DH:(g + 1) * GROUP * C_DH,
                                 c * CHUNK:(c + 1) * CHUNK].rearrange("(h d) n -> d h n", d=C_DH)
                    ).then_inc(q_stacked[g], 16)

            def stack_max(G):
                sp.wait_ge(maxT_copied, G + 1)
                for k in range(LEVELS):
                    sp.dma_start(qstack[SROWS + k:SROWS + k + 1, buffer(G), :, :],
                                 maxT[GROUP * k:GROUP * k + GROUP, G % 2, :]).then_inc(max_stacked, 16)

            for c in range(CHUNKS):
                sp.wait_ge(q_split, c + 1)
                sp.dma_start(qparts_d[:, :, c * CHUNK:(c + 1) * CHUNK].rearrange("k (f p) n -> p (k f) n", p=P),
                             qpart.rearrange("p k (f n) -> p (k f) n", f=DK)).then_inc(q_written, 16)
                if c == 0:
                    sp.wait_ge(q_written, 16)
                    for G in range(GROUPS - 1):
                        stack_queries(G)

            n = CHUNKS * GROUPS
            for G in range(n + 2):
                if GROUPS - 1 <= G < n:
                    stack_queries(G)
                if G >= 2:
                    stack_max(G - 2)
                if G == 2:
                    sp.wait_ge(vc_ready, KT)
                    for e in range(W_SLOTS):
                        load_weights(e)
            for e in range(W_SLOTS, FFN):
                load_weights(e)
            for t in range(TILES):
                sp.wait_ge(out_ready, t + 1)
                sp.dma_start(out[t * P:(t + 1) * P, :], x_sb[:, t, :]).then_inc(out_written, 16)
            sp.wait_ge(out_written, 16 * TILES)

        @block.gpsimd
        def _(pool):
            n = [0]

            def link(ins):
                n[0] += 1
                ins.then_inc(pool_step, 1)
                pool.wait_ge(pool_step, n[0])

            pool.memset(context, 0.0).then_inc(zeros_ready, 1)
            link(pool.memset(ident[:, :], 0.0))
            link(pool.memset(half_neg[:, :], -0.5))
            link(pool.affine_select(out=ident[:, :], in_=ident[:, :], compare_op=ALU.not_equal, fill=1.0,
                                    base=0, pattern=[[-1, P]], channel_multiplier=1))
            pool.tensor_copy(ident_b[:, :], ident[:, :]).then_inc(consts_ready, 1)
            link(pool.memset(sel_f[:, :], 0.0))
            for part in range(2):
                link(pool.affine_select(out=sel_f[:, :], in_=sel_f[:, :], compare_op=ALU.not_equal, fill=1.0,
                                        base=-EXPERTS * part, pattern=[[-1, EXPERTS]], channel_multiplier=1))
            pool.tensor_copy(expert_sel[:, :], sel_f[:, :]).then_inc(sel_ready, 1)
            pool.memset(zero_gate[:, :, :], 0.0).then_inc(zero_ready, 1)
            pool.wait_ge(ld_x, 16)
            pool.wait_ge(ld_bias, 16 * 7)
            for t in range(TILES):
                pool.tensor_tensor(x_sb[:, t, :], x_sb[:, t, :], bo_row[:, :], ALU.add).then_inc(x_biased, 1)
            pool.wait_ge(ctx_ready, 1)
            link(pool.memset(vals, 0.0))
            pool.memset(vals[:, :, :, C_DH:C_DH + 1], 1.0).then_inc(zeros_ready, 1)
            pool.wait_ge(zeros_ready, 2)
            pool.memset(region1[SROWS:SROWS + LEVELS, 0:KW], 1.0 + 0x3F80 * 2.0 ** -23).then_inc(zeros_ready, 1)
            pool.wait_ge(zeros_ready, 3)

            def inverse_deviation(var, done, t, w):
                pool.wait_ge(var, t + 1)
                at = t % TPC if w == 1 else 0
                pool.tensor_tensor(rstd[:, at:at + w], var_eps[:, at:at + w], half_neg[:, 0:w],
                                   ALU.pow).then_inc(done, 1)

            def second_part_x2(c, k):
                pool.wait_ge(x2_hi_ready, DK * c + k + 1)
                part = (slice(None), k, slice(c * CHUNK, (c + 1) * CHUNK))
                pool.tensor_tensor(x2_lo[part], attnT[:, k, :], x2_hi[part].bitcast(F32),
                                   ALU.subtract).then_inc(x2_lo_ready, 1)

            def second_part_w(e):
                pool.wait_ge(w_hi_ready, e + 1)
                pool.tensor_tensor(w_lo[:, e, :], w_raw[:, e % W_SLOTS, :], w_hi[:, e, :].bitcast(F32),
                                   ALU.subtract).then_inc(w_lo_ready, 1)

            for t in range(TILES):
                inverse_deviation(b_var, b_rstd, t, 1)
            for t in range(TILES):
                pool.wait_ge(x1T_ready, t + 1)
                pool.tensor_tensor(x_sb[:, t, :], x_sb[:, t, :], boc_row[:, :], ALU.add).then_inc(x1_biased, 1)
            for c in range(CHUNKS - 1):
                inverse_deviation(c_var, c_rstd, c, TPC)
                for k in range(DK):
                    second_part_x2(c, k)
            for e in range(FFN):
                second_part_w(e)
                if e == 6:
                    inverse_deviation(c_var, c_rstd, CHUNKS - 1, TPC)
                if e in (8, 9):
                    second_part_x2(CHUNKS - 1, e - 8)
            for c in range(CHUNKS):
                inverse_deviation(d_var, d_rstd, c, TPC)

        @block.scalar
        def _(act):
            act.dma_start(wk_s, a["L0_attn_Wk"].rearrange("(k p) n -> p k n", p=P)).then_inc(ld_wk, 16)
            act.dma_start(x_sb[:, :, :], a["x"].rearrange("(t p) n -> p t n", p=P)).then_inc(ld_x, 16)
            act.dma_start(wo_s, a["L0_attn_Wo"].rearrange("(f p) n -> p f n", p=P)).then_inc(ld_wo, 16)
            act.dma_start(bo_row[:, :], a["L0_attn_bo"].rearrange("(a n) -> a n", a=1).broadcast_to([P, DIM])).then_inc(ld_bias, 16)
            act.dma_start(bv_row[:, :], a["L0_xattn_bv"].rearrange("(a n) -> a n", a=1).broadcast_to([P, DIM])).then_inc(ld_bias, 16)
            act.dma_start(boc_row[:, :], a["L0_xattn_bo"].rearrange("(a n) -> a n", a=1).broadcast_to([P, DIM])).then_inc(ld_bias, 16)
            act.dma_start(bq_c[:, :], a["bq2"]).then_inc(ld_bias, 16)
            act.dma_start(bk_c[:, :], a["bk2"]).then_inc(ld_bias, 16)
            for k in range(DK):
                act.dma_start(gate_wT[:, k, :], a["gateT"][k * P:(k + 1) * P, :]).then_inc(ld_bias, 16)

            for f in range(SF):
                act.wait_ge(kmax_ready, f + 1)
                act.activation(ekT[:, f, :], bank(4 * (f % 2), 4), ACT.Exp, bias=nkmax[:, f:f + 1],
                               accum_out=ksum[:, f:f + 1]).then_inc(k_exp, 1)
            for t in range(TILES):
                act.wait_ge(ekT_ready, t + 1)
                act.activation(ek[:, t, :], bank(4 + t % 2), ACT.Copy).then_inc(ek_copied, 1)
            act.wait_ge(ld_bias, 16 * 7)
            for f in range(DK):
                act.wait_ge(kc_ready, f + 1)
                act.activation(kf[:, f, :], psum[:, 4 * f * CHUNK:4 * f * CHUNK + KEYS], ACT.Identity,
                               bias=bk_c[:, f:f + 1]).then_inc(kc_copied, 1)

            for i in range(TILES + 13):
                if i < TILES:
                    act.wait_ge(q_centred, i + 1)
                    act.activation(qexp[:, i % 2, :], qexp[:, i % 2, :], ACT.Exp).then_inc(q_exp, 1)
                t = i - 2
                if 0 <= t < TILES:
                    act.wait_ge(qT_ready, t + 1)
                    if t >= 2:
                        act.wait_ge(y_ready, t - 1)
                    act.activation(qsT[:, t % 2, :], bank(2 + t % 2), ACT.Copy).then_inc(qT_copied, 1)
                t = i - 6
                if 0 <= t < TILES:
                    act.wait_ge(x1T_ready, t + 1)
                    act.activation(xT[:, :, t * P:(t + 1) * P],
                                   bank(5)[:, 0:DK * P].rearrange("p (k n) -> p k n", k=DK),
                                   ACT.Copy).then_inc(x1T_copied, 1)
                if (i - 11) % TPC == 0 and 0 <= (i - 11) // TPC < CHUNKS:
                    c = (i - 11) // TPC
                    act.wait_ge(qp_ready, c + 1)
                    if c >= 1:
                        act.wait_ge(q_split, c)
                    for f in range(DK):
                        act.activation(qf[:, f * CHUNK:(f + 1) * CHUNK], bank(6 + f), ACT.Identity,
                                       bias=bq_c[:, f:f + 1]).then_inc(qf_copied, 1)

            def copy_max(G):
                act.wait_ge(maxT_ready, G + 1)
                if G >= 2:
                    act.wait_ge(max_stacked, 16 * LEVELS * (G - 1))
                act.activation(maxT[:, G % 2, :], bank(5).bitcast(BF16)[0:LEVELS * GROUP, 0:CHUNK],
                               ACT.Copy).then_inc(maxT_copied, 1)

            def copy_num(G):
                act.wait_ge(pv_done, KT * (G + 1))
                if G >= 1:
                    act.wait_ge(den_ready, G)
                act.activation(numT[:, :], bank(4), ACT.Copy).then_inc(num_copied, 1)

            def copy_attnT(c, k):
                act.wait_ge(attnT_ready, DK * c + k + 1)
                if c >= 1:
                    act.wait_ge(logits_ready, c)
                    act.wait_ge(x2_lo_ready, DK * c)
                act.activation(attnT[:, k, :], bank(5), ACT.Copy).then_inc(attnT_copied, 1)

            def copy_x2T(c, k):
                act.wait_ge(x2T_ready, DK * c + k + 1)
                if k == 0:
                    act.wait_ge(co_ready, 2 * (c + 1))
                act.activation(attnT[:, k, :], bank(5), ACT.Copy).then_inc(x2T_copied, 1)
                act.wait_ge(x2T_copied, DK * c + k + 1)
                act.activation(x2_hi[:, k, c * CHUNK:(c + 1) * CHUNK], attnT[:, k, :], ACT.Copy).then_inc(x2_hi_ready, 1)

            def copy_logits(c):
                act.wait_ge(logits_ready, c + 1)
                act.activation(logits[:, TPC * c:TPC * (c + 1), :].rearrange("p t e -> p (t e)"),
                               bank(5)[:, 0:TPC * EXPERTS], ACT.Copy).then_inc(logits_copied, 1)

            def exp_gate(call, lo, hi):
                act.wait_ge(gate_centred, call)
                act.activation(gate_work[:, lo:hi, :], gate_work[:, lo:hi, :], ACT.Exp).then_inc(gate_exp, 1)

            def first_part_w(e):
                act.wait_ge(ld_w[e % W_SLOTS], 16 * 3 * (e // W_SLOTS + 1))
                act.activation(w_hi[:, e, :], w_raw[:, e % W_SLOTS, :], ACT.Copy).then_inc(w_hi_ready, 1)

            copy_max(0)
            act.wait_ge(q_written, 16 * CHUNKS)
            for G in range(CHUNKS * GROUPS):
                c, g = divmod(G, GROUPS)
                for kt in range(KT):
                    s = KT * G + kt
                    r = krows(kt)
                    if s >= 3:
                        act.wait_ge(pv_done, s - 2)
                    if kt == 1 and G >= 1:
                        copy_num(G - 1)
                    for j in range(GROUP):
                        n = GROUP * s + j
                        act.wait_ge(st_ready, n + 1)
                        act.activation(prob[0:r, s % 3, j, :], bank(n % ST_BANKS)[0:r],
                                       ACT.Exp).then_inc(p_ready, 1)
                    if g == 0 and c >= 1 and kt in (4, 5):
                        copy_attnT(c - 1, kt - 4)
                    if g == 1 and c >= 1 and kt in (4, 5):
                        copy_x2T(c - 1, kt - 4)
                    if g == 1 and c >= 1 and kt == 7:
                        copy_logits(c - 1)
                    if G == CHUNKS * GROUPS - 1 and kt == 6:
                        exp_gate(1, 0, GATE_FIRST)
                    if kt == 11 and G + 1 < CHUNKS * GROUPS:
                        copy_max(G + 1)
            copy_num(CHUNKS * GROUPS - 1)
            act.wait_ge(pv_done, STEPS)
            for e in range(AHEAD):
                first_part_w(e)
            act.wait_ge(gate_turned, 1)
            act.activation(comb[0:2 * EXPERTS, 0:CHUNK], bank(3)[0:2 * EXPERTS], ACT.Copy).then_inc(comb_copied, 1)
            act.activation(comb[0:2 * EXPERTS, CHUNK:3 * CHUNK], bank(6, 2)[0:2 * EXPERTS],
                           ACT.Copy).then_inc(comb_copied, 1)

            def copy_ffn(c):
                act.wait_ge(act_done, FFN * (c + 1))
                if c == 0:
                    act.wait_ge(logits_ready, CHUNKS)
                    act.wait_ge(x2_lo_ready, DK * CHUNKS)
                else:
                    act.wait_ge(ffnN_ready, 2 * c)
                for d in range(DK):
                    act.activation(ffnT[:, d, :], bank(6 + d), ACT.Copy).then_inc(ffn_copied, 1)

            for i in range(CHUNKS * FFN):
                c, e = divmod(i, FFN)
                if e < EXPERTS:
                    act.wait_ge(blend_ready, EXPERTS * c + e + 1)
                    if i >= 1:
                        act.wait_ge(weighted_ready, i)
                    act.activation(blend_s[:, :], bank(4), ACT.Copy, scale=0.5).then_inc(blend_copied, 1)
                act.wait_ge(h_ready, i + 1)
                if i >= 2:
                    act.wait_ge(h_read, i - 1)
                act.activation(tanh_h[:, i % 2, :], bank(2 * (i % 2)), ACT.Tanh, scale=0.5).then_inc(tanh_ready, 1)
                if c == 0 and e + AHEAD < FFN:
                    first_part_w(e + AHEAD)
                act.wait_ge(act_ready, i + 1)
                if i >= 2:
                    act.wait_ge(act_done, i - 1)
                    act.wait_ge(act_lo_ready, i - 1)
                act.activation(act_hi[:, i % 2, :], act_h[:, i % 2, :], ACT.Copy).then_inc(act_hi_ready, 1)
                if c >= 1 and e == 0:
                    copy_ffn(c - 1)
                if i in (1, 2):
                    copy_attnT(CHUNKS - 1, i - 1)
                if i in (6, 7):
                    copy_x2T(CHUNKS - 1, i - 6)
                if i == 8:
                    copy_logits(CHUNKS - 1)
                if i == 9:
                    exp_gate(2, GATE_FIRST, TILES)
                if i == 12:
                    act.wait_ge(gate_turned, 2)
                    act.activation(comb[0:2 * EXPERTS, 3 * CHUNK:SEQ], bank(5)[0:2 * EXPERTS],
                                   ACT.Copy).then_inc(comb_copied, 1)
            copy_ffn(CHUNKS - 1)

        @block.tensor
        def _(pe):
            pe.wait_ge(ld_wk, 16)
            pe.wait_ge(ld_xT, 16)
            for f in range(SF):
                if f >= 2:
                    pe.wait_ge(k_exp, f - 1)
                for n in range(SEQ // CHUNK):
                    for k in range(DK):
                        mm = pe.matmul(bank(4 * (f % 2) + n), wk_s[:, k, f * P:(f + 1) * P],
                                       xT[:, k, n * CHUNK:(n + 1) * CHUNK], start=(k == 0), stop=(k == DK - 1))
                mm.then_inc(kT_ready, 1)
            pe.wait_ge(ld_wv, 16)
            pe.wait_ge(consts_ready, 1)
            pe.wait_ge(k_exp, 3)
            for t in range(TILES + 1):
                if t < TILES:
                    if t >= 4:
                        pe.wait_ge(v_copied, t - 3)
                    for k in range(DK):
                        mm = pe.matmul(bank(t % 4), xT[:, k, t * P:(t + 1) * P], wv_s[:, k, :],
                                       start=(k == 0), stop=(k == DK - 1))
                    mm.then_inc(v_ready, 1)
                if t >= 1:
                    u = t - 1
                    pe.wait_ge(k_exp, 4)
                    if u >= 2:
                        pe.wait_ge(ek_copied, u - 1)
                    for f in range(SF):
                        mm = pe.transpose(bank(4 + u % 2)[:, f * P:(f + 1) * P], ekT[:, f, u * P:(u + 1) * P],
                                          ident[:, :])
                    mm.then_inc(ekT_ready, 1)
            pe.wait_ge(v_copied, TILES)
            pe.wait_ge(ek_copied, TILES)
            for f in range(SF):
                for t in range(TILES):
                    mm = pe.matmul(bank(6)[:, f * P:(f + 1) * P], v_s[:, t, f * P:(f + 1) * P],
                                   ek[:, t, f * P:(f + 1) * P], start=(t == 0), stop=(t == TILES - 1))
            mm.then_inc(ctx_ready, 1)
            pe.wait_ge(ld_ctx, 16)
            pe.wait_ge(ld_cw, 16 * 3)
            for f in range(DK):
                if f == 1:
                    pe.wait_ge(fold_copied, 1)
                for n in range(0, KEYS, CHUNK):
                    w = min(CHUNK, KEYS - n)
                    for k in range(DK):
                        mm = pe.matmul(bank(4 * f + n // CHUNK)[:, 0:w], wk_c[:, k, f * P:(f + 1) * P],
                                       ctxT[:, k, n:n + w], start=(k == 0), stop=(k == DK - 1))
                mm.then_inc(kc_ready, 1)
                if f == 0:
                    pe.wait_ge(ctx_copied, 2)
                    pe.wait_ge(ld_wo, 16)
                    for j in range(SF):
                        mm = pe.matmul(bank(4 + j // 2)[:, (j % 2) * DIM:(j % 2 + 1) * DIM], context[:, j, :],
                                       wo_s[:, j, :], start=True, stop=True)
                    mm.then_inc(fold_ready, 1)
            pe.wait_ge(ld_wq, 16)
            pe.wait_ge(kc_copied, 2)
            for i in range(TILES + 13):
                if i < TILES:
                    if i >= 2:
                        pe.wait_ge(q_centred, i - 1)
                    for k in range(DK):
                        mm = pe.matmul(bank(i % 2), xT[:, k, i * P:(i + 1) * P], wq_s[:, k, :],
                                       start=(k == 0), stop=(k == DK - 1))
                    mm.then_inc(q_ready, 1)
                t = i - 2
                if 0 <= t < TILES:
                    pe.wait_ge(qn_ready, t + 1)
                    if t >= 2:
                        pe.wait_ge(qT_copied, t - 1)
                    for f in range(SF):
                        mm = pe.transpose(bank(2 + t % 2)[:, f * P:(f + 1) * P],
                                          qnorm[:, t % 2, f * P:(f + 1) * P], ident[:, :])
                    mm.then_inc(qT_ready, 1)
                t = i - 3
                if 0 <= t < TILES:
                    pe.wait_ge(qT_copied, t + 1)
                    if t >= 1:
                        pe.wait_ge(y_read, t)
                    for f in range(SF):
                        mm = pe.matmul(bank(4)[:, 0:DIM], qsT[:, t % 2, f * P:(f + 1) * P], fold[:, f, :],
                                       start=(f == 0), stop=(f == SF - 1))
                    mm.then_inc(y_ready, 1)
                t = i - 6
                if 0 <= t < TILES:
                    pe.wait_ge(x1_ready, t + 1)
                    if t >= 1:
                        pe.wait_ge(x1T_copied, t)
                    for k in range(DK):
                        mm = pe.transpose(bank(5)[:, k * P:(k + 1) * P], x_sb[:, t, k * P:(k + 1) * P], ident[:, :])
                    mm.then_inc(x1T_ready, 1)
                if (i - 10) % TPC == 0 and 0 <= (i - 10) // TPC < CHUNKS:
                    c = (i - 10) // TPC
                    pe.wait_ge(x1T_copied, TPC * (c + 1))
                    if c >= 1:
                        pe.wait_ge(qf_copied, DK * c)
                    for f in range(DK):
                        for k in range(DK):
                            mm = pe.matmul(bank(6 + f), wq_c[:, k, f * P:(f + 1) * P],
                                           xT[:, k, c * CHUNK:(c + 1) * CHUNK], start=(k == 0), stop=(k == DK - 1))
                    mm.then_inc(qp_ready, 1)
                t = i - TILES
                if 0 <= t < KT:
                    if t == 0:
                        pe.wait_ge(q_centred, TILES)
                    if t >= 2:
                        pe.wait_ge(vc_copied, t - 1)
                    r = krows(t)
                    for k in range(DK):
                        mm = pe.matmul(bank(t % 2)[0:r, 0:DIM], ctxT[:, k, t * P:t * P + r], wv_c[:, k, :],
                                       start=(k == 0), stop=(k == DK - 1))
                    mm.then_inc(vc_ready, 1)

            def max_unit(u):
                G, v = divmod(u, UNITS)
                qt, rest = divmod(v, GROUP * PIECES)
                j, n = divmod(rest, PIECES)
                g = G % GROUPS
                at, w = piece(n)
                if v == 0:
                    pe.wait_ge(q_stacked[g], 16 * SPLIT * (G // GROUPS + 1))
                if u >= len(MAX_BANKS):
                    pe.wait_ge(max_read, u - len(MAX_BANKS) + 1)
                pe.matmul(bank(MAX_BANKS[u % len(MAX_BANKS)])[:, 0:w], qstack[0:SROWS, buffer(G), j, qt * P:(qt + 1) * P],
                          kstack[0:SROWS, g * GROUP + j, at:at + w], start=True, stop=True).then_inc(max_scores, 1)

            def turn_max(G):
                pe.wait_ge(max_split, G + 1)
                if G >= 1:
                    pe.wait_ge(maxT_copied, G)
                for t in range(TPC):
                    mm = pe.transpose(bank(5).bitcast(BF16)[0:LEVELS * GROUP, t * P:(t + 1) * P],
                                      mlev[:, t, :, :].rearrange("p k h -> p (k h)"), ident_b[:, :])
                mm.then_inc(maxT_ready, 1)

            def scores(s, j):
                G, kt = divmod(s, KT)
                g, r = G % GROUPS, krows(kt)
                n = GROUP * s + j
                if kt == 0 and j == 0:
                    pe.wait_ge(max_stacked, 16 * LEVELS * (G + 1))
                if n >= ST_BANKS:
                    pe.wait_ge(p_ready, n - ST_BANKS + 1)
                pe.matmul(bank(n % ST_BANKS)[0:r], kstack[0:SROWS + LEVELS, g * GROUP + j, kt * P:kt * P + r],
                          qstack[0:SROWS + LEVELS, buffer(G), j, :], start=True, stop=True).then_inc(st_ready, 1)

            def weigh(s):
                G, kt = divmod(s, KT)
                g, r = G % GROUPS, krows(kt)
                pe.wait_ge(p_ready, GROUP * (s + 1))
                if kt == 0 and G >= 1:
                    pe.wait_ge(num_copied, G)
                for j in range(GROUP):
                    mm = pe.matmul(bank(4)[VW * j:VW * (j + 1)], vals[0:r, kt, g * GROUP + j, :],
                                   prob[0:r, s % 3, j, :], start=(kt == 0), stop=(kt == KT - 1))
                mm.then_inc(pv_done, 1)

            def turn_num(G):
                pe.wait_ge(num_copied, G + 1)
                if G + 1 < CHUNKS * GROUPS:
                    pe.wait_ge(maxT_copied, G + 2)
                else:
                    pe.wait_ge(attn_ready, G)
                for t in range(TPC):
                    mm = pe.transpose(bank(5)[:, t * P:(t + 1) * P], numT[:, t * P:(t + 1) * P], ident[:, :])
                mm.then_inc(den_ready, 1)

            def turn_attn(c, k):
                pe.wait_ge(attn_ready, GROUPS * (c + 1))
                if k >= 1:
                    pe.wait_ge(attnT_copied, DK * c + k)
                for t in range(TPC):
                    mm = pe.transpose(bank(5)[:, t * P:(t + 1) * P],
                                      attn[:, t, 2 * k:2 * k + 2, :, :].rearrange("p g h d -> p (g h d)"), ident[:, :])
                mm.then_inc(attnT_ready, 1)

            def out_proj(c, half):
                n = 2 * c + half
                pe.wait_ge(attnT_copied, DK * (c + 1))
                if half == 1:
                    pe.wait_ge(co_read, n)
                if n == 0:
                    pe.wait_ge(ld_woc, 16)
                for q in range(2):
                    t = 2 * half + q
                    for k in range(DK):
                        mm = pe.matmul(bank(5)[:, q * DIM:(q + 1) * DIM], attnT[:, k, t * P:(t + 1) * P],
                                       wo_c[:, k, :], start=(k == 0), stop=(k == DK - 1))
                mm.then_inc(co_ready, 1)

            def turn_x2(c, k):
                pe.wait_ge(x2_ready, TPC * (c + 1))
                if k == 0 and c + 1 < CHUNKS:
                    pe.wait_ge(attn_ready, GROUPS * (c + 1) + 1)
                if k >= 1:
                    pe.wait_ge(x2T_copied, DK * c + k)
                for t in range(TPC):
                    mm = pe.transpose(bank(5)[:, t * P:(t + 1) * P],
                                      x_sb[:, TPC * c + t, k * P:(k + 1) * P], ident[:, :])
                mm.then_inc(x2T_ready, 1)

            def gate_logits(c):
                pe.wait_ge(x2T_copied, DK * (c + 1))
                if c == 0:
                    pe.wait_ge(ld_bias, 16 * 7)
                for t in range(TPC):
                    for k in range(DK):
                        mm = pe.matmul(bank(5)[:, t * EXPERTS:(t + 1) * EXPERTS], attnT[:, k, t * P:(t + 1) * P],
                                       gate_wT[:, k, :], start=(k == 0), stop=(k == DK - 1))
                mm.then_inc(logits_ready, 1)

            def turn_gate(call, lo, hi, banks):
                pe.wait_ge(gate_ready, call)
                for t in range(lo, hi):
                    n = t - lo
                    mm = pe.transpose(bank(banks[n // TPC])[0:2 * EXPERTS, n % TPC * P:(n % TPC + 1) * P],
                                      gate_parts[:, t, :, :].bitcast(F32).rearrange("p a e -> p (a e)"), ident[:, :])
                mm.then_inc(gate_turned, 1)

            pe.wait_ge(qf_copied, DK * CHUNKS)
            pe.wait_ge(vc_copied, KT)
            pe.wait_ge(k_stacked, 16 * SPLIT)
            pe.wait_ge(zeros_ready, 3)
            for u in range(units_until(-1)):
                max_unit(u)
                if u == UNITS + SPLIT_STEPS + 2:
                    turn_max(0)
            for s in range(STEPS):
                G, kt = divmod(s, KT)
                c, g = divmod(G, GROUPS)
                units = list(range(units_until(s - 1), units_until(s)))
                for u in units[0:1]:
                    max_unit(u)
                scores(s, 0)
                scores(s, 1)
                for u in units[1:2]:
                    max_unit(u)
                scores(s, 2)
                for u in units[2:3]:
                    max_unit(u)
                if s >= 1:
                    weigh(s - 1)
                scores(s, 3)
                for u in units[3:]:
                    max_unit(u)
                if kt == 2 and G >= 1:
                    turn_num(G - 1)
                if g == 0 and c >= 1:
                    if kt in (4, 5):
                        turn_attn(c - 1, kt - 4)
                    if kt in (6, 7):
                        out_proj(c - 1, kt - 6)
                if g == 1 and c >= 1 and kt in (4, 5):
                    turn_x2(c - 1, kt - 4)
                if g == 1 and c >= 1 and kt == 6:
                    gate_logits(c - 1)
                if kt == 11 and G + 1 < CHUNKS * GROUPS:
                    if g == 0 and c >= 1:
                        pe.wait_ge(co_read, 2 * c)
                    elif g == 1 and c >= 1:
                        pe.wait_ge(logits_copied, c)
                    elif G >= 1:
                        pe.wait_ge(attn_ready, G)
                    turn_max(G + 1)
            weigh(STEPS - 1)
            turn_gate(1, 0, GATE_FIRST, MAX_BANKS)
            pe.wait_ge(sel_ready, 1)

            def blend(i):
                c, e = divmod(i, FFN)
                if e == 0:
                    pe.wait_ge(comb_copied, 3 if c == CHUNKS - 1 else 2)
                if i == 0:
                    pe.wait_ge(num_copied, CHUNKS * GROUPS)
                elif e < EXPERTS:
                    pe.wait_ge(blend_copied, EXPERTS * c + e)
                if e < EXPERTS:
                    pe.matmul(bank(4), expert_sel[0:2 * EXPERTS, e:e + 1].broadcast_to([2 * EXPERTS, P]),
                              comb[0:2 * EXPERTS, c * CHUNK:(c + 1) * CHUNK],
                              start=True, stop=True).then_inc(blend_ready, 1)

            def hidden(i):
                c, e = divmod(i, FFN)
                if i >= 2:
                    pe.wait_ge(h_read, i - 1)
                if c == 0:
                    pe.wait_ge(w_lo_ready, e + 1)
                if e == 0:
                    pe.wait_ge(x2_lo_ready, DK * (c + 1))
                for b in range(2):
                    for k in range(DK):
                        col = slice((b * DK + k) * HID, (b * DK + k + 1) * HID)
                        tok = (slice(None), k, slice(c * CHUNK, (c + 1) * CHUNK))
                        out_bank = bank(2 * (i % 2) + b)
                        pe.matmul(out_bank, w_hi[:, e, col], x2_hi[tok], start=(k == 0), stop=False)
                        pe.matmul(out_bank, w_hi[:, e, col], x2_lo[tok], start=False, stop=False)
                        mm = pe.matmul(out_bank, w_lo[:, e, col], x2_hi[tok], start=False, stop=(k == DK - 1))
                mm.then_inc(h_ready, 1)

            def second(i):
                c, e = divmod(i, FFN)
                if e == 0 and c >= 1:
                    pe.wait_ge(ffn_copied, DK * c)
                pe.wait_ge(act_hi_ready, i + 1)
                cols = [slice(2 * DK * HID + d * P, 2 * DK * HID + (d + 1) * P) for d in range(DK)]
                for d in range(DK):
                    pe.matmul(bank(6 + d), w_hi[:, e, cols[d]], act_hi[:, i % 2, :], start=(e == 0), stop=False)
                    pe.matmul(bank(6 + d), w_lo[:, e, cols[d]], act_hi[:, i % 2, :], start=False, stop=False)
                pe.wait_ge(act_lo_ready, i + 1)
                for d in range(DK):
                    mm = pe.matmul(bank(6 + d), w_hi[:, e, cols[d]], act_lo[:, i % 2, :],
                                   start=False, stop=(e == FFN - 1))
                mm.then_inc(act_done, 1)

            def turn_ffn(c, half):
                n = 2 * c + half
                pe.wait_ge(ffn_copied, DK * (c + 1))
                if n >= 1:
                    pe.wait_ge(ffnN_read, n)
                else:
                    pe.wait_ge(comb_copied, 3)
                for q in range(2):
                    t = 2 * half + q
                    for d in range(DK):
                        mm = pe.transpose(bank(5)[:, q * DIM + d * P:q * DIM + (d + 1) * P],
                                          ffnT[:, d, t * P:(t + 1) * P], ident[:, :])
                mm.then_inc(ffnN_ready, 1)

            for i in range(CHUNKS * FFN + 1):
                c, e = divmod(i, FFN)
                if i < CHUNKS * FFN:
                    blend(i)
                    hidden(i)
                if i >= 1:
                    second(i - 1)
                if i == 0:
                    turn_num(CHUNKS * GROUPS - 1)
                if i in (1, 2):
                    turn_attn(CHUNKS - 1, i - 1)
                if i in (3, 4):
                    out_proj(CHUNKS - 1, i - 3)
                if i in (6, 7):
                    turn_x2(CHUNKS - 1, i - 6)
                if i == 8:
                    gate_logits(CHUNKS - 1)
                if i == 12:
                    turn_gate(2, GATE_FIRST, TILES, (5,))
                if c >= 1 and c < CHUNKS and e in (2, 4):
                    turn_ffn(c - 1, e // 2 - 1)
            for half in range(2):
                turn_ffn(CHUNKS - 1, half)

        @block.vector
        def _(dve):
            n = [0]

            def link(ins):
                n[0] += 1
                ins.then_inc(vec_step, 1)
                dve.wait_ge(vec_step, n[0])

            for f in range(SF):
                dve.wait_ge(kT_ready, f + 1)
                dve.tensor_reduce(nkmax[:, f:f + 1], bank(4 * (f % 2), 4), X, ALU.max, negate=True).then_inc(kmax_ready, 1)
            for t in range(TILES):
                dve.wait_ge(v_ready, t + 1)
                dve.tensor_copy(v_s[:, t, :], bank(t % 4)).then_inc(v_copied, 1)
            dve.wait_ge(k_exp, SF)
            link(dve.reciprocal(krec[:, :], ksum[:, :]))
            dve.wait_ge(ctx_ready, 1)
            dve.wait_ge(zeros_ready, 1)
            for half in (0, S_DH):
                dve.tensor_copy(context[half:half + S_DH, :, half:half + S_DH],
                                bank(6)[half:half + S_DH, :].rearrange("p (f n) -> p f n", f=SF)
                                [:, :, half:half + S_DH]).then_inc(ctx_copied, 1)
            dve.wait_ge(fold_ready, 1)
            for j in range(SF):
                ins = dve.tensor_scalar(fold[:, j, :], bank(4 + j // 2)[:, (j % 2) * DIM:(j % 2 + 1) * DIM],
                                        krec[:, j:j + 1], S_SCALE, ALU.mult, ALU.mult)
            ins.then_inc(fold_copied, 1)
            for f in range(DK):
                dve.wait_ge(kc_copied, f + 1)
                link(dve.tensor_scalar(kf[:, f, :], kf[:, f, :], C_SCALE, None, ALU.mult))
                link(dve.tensor_copy(kpart[:, 0, f, :], kf[:, f, :]))
                link(dve.tensor_tensor(kres, kf[:, f, :], kpart[:, 0, f, :], ALU.subtract))
                link(dve.tensor_copy(kpart[:, 1, f, :], kres))
                link(dve.tensor_tensor(kres, kres, kpart[:, 1, f, :], ALU.subtract))
                ins = dve.tensor_copy(kpart[:, 2, f, :], kres)
                if f == DK - 1:
                    ins.then_inc(k_split, 1)
                else:
                    link(ins)
            dve.wait_ge(k_written, 16 * LEVELS)

            def norm_stats(r, at, last, signal):
                link(dve.bn_stats(stats[:, at, :], r))
                link(dve.bn_aggr(meanvar[:, at, :], stats[:, at, :]))

            qmax = [small[:, 32 * b:32 * b + S_HEADS] for b in range(2)]
            qsum = [small[:, 32 * b + 8:32 * b + 8 + S_HEADS] for b in range(2)]
            qrec = [small[:, 32 * b + 16:32 * b + 16 + S_HEADS] for b in range(2)]

            def heads(ap):
                return ap.rearrange("p (h d) -> p h d", h=S_HEADS)

            def spread(ap):
                return ap.rearrange("p (h o) -> p h o", o=1).broadcast_to([P, S_HEADS, S_DH])

            for i in range(TILES + 13):
                t = i - 4
                if 0 <= t < TILES:
                    dve.wait_ge(y_ready, t + 1)
                    dve.wait_ge(x_biased, t + 1)
                    if t >= 2:
                        dve.wait_ge(x1_ready, t - 1)
                    dve.tensor_tensor(resid[:, t % 2, :], bank(4)[:, 0:DIM], x_sb[:, t, :], ALU.add).then_inc(y_read, 1)
                    dve.wait_ge(y_read, t + 1)
                    norm_stats(resid[:, t % 2, :], t % TPC, None, None)
                    dve.tensor_scalar(var_eps[:, t % TPC:t % TPC + 1], meanvar[:, t % TPC, 1:2], EPS, None,
                                      ALU.add).then_inc(b_var, 1)
                t = i - 5
                if 0 <= t < TILES:
                    dve.wait_ge(b_rstd, t + 1)
                    dve.tensor_scalar(x_sb[:, t, :], resid[:, t % 2, :], meanvar[:, t % TPC, 0:1],
                                      rstd[:, t % TPC:t % TPC + 1], ALU.subtract, ALU.mult).then_inc(x1_ready, 1)
                if i < TILES:
                    dve.wait_ge(q_ready, i + 1)
                    if i >= 2:
                        dve.wait_ge(q_centred, i - 1)
                        dve.wait_ge(qn_ready, i - 1)
                    link(dve.tensor_reduce(qmax[i % 2], heads(bank(i % 2)), X, ALU.max))
                    dve.tensor_tensor(heads(qexp[:, i % 2, :]), heads(bank(i % 2)), spread(qmax[i % 2]),
                                      ALU.subtract).then_inc(q_centred, 1)
                t = i - 1
                if 0 <= t < TILES:
                    dve.wait_ge(q_exp, t + 1)
                    link(dve.tensor_reduce(qsum[t % 2], heads(qexp[:, t % 2, :]), X, ALU.add))
                    link(dve.reciprocal(qrec[t % 2], qsum[t % 2]))
                    if t >= 2:
                        dve.wait_ge(qT_ready, t - 1)
                    dve.tensor_tensor(heads(qnorm[:, t % 2, :]), heads(qexp[:, t % 2, :]), spread(qrec[t % 2]),
                                      ALU.mult).then_inc(qn_ready, 1)
                t = i - TILES
                if 0 <= t < KT:
                    r = krows(t)
                    if t == 0:
                        dve.wait_ge(zeros_ready, 3)
                        dve.wait_ge(ld_bias, 16 * 7)
                    dve.wait_ge(vc_ready, t + 1)
                    dve.tensor_tensor(vals[0:r, t, :, 0:C_DH],
                                      bank(t % 2)[0:r, 0:DIM].rearrange("p (h d) -> p h d", h=C_HEADS),
                                      bv_row[0:r, :].rearrange("p (h d) -> p h d", h=C_HEADS),
                                      ALU.add).then_inc(vc_copied, 1)
                if (i - 12) % TPC == 0 and 0 <= (i - 12) // TPC < CHUNKS:
                    c = (i - 12) // TPC
                    dve.wait_ge(qf_copied, DK * (c + 1))
                    if c >= 1:
                        dve.wait_ge(q_written, 16 * c)
                    link(dve.tensor_copy(qpart[:, 0, :], qf))
                    link(dve.tensor_tensor(qres, qf, qpart[:, 0, :], ALU.subtract))
                    link(dve.tensor_copy(qpart[:, 1, :], qres))
                    link(dve.tensor_tensor(qres, qres, qpart[:, 1, :], ALU.subtract))
                    dve.tensor_copy(qpart[:, 2, :], qres).then_inc(q_split, 1)

            def read_max(u):
                w = piece(u % PIECES)[1]
                dve.wait_ge(max_scores, u + 1)
                v = u % UNITS
                dve.tensor_reduce(mpart[:, u // UNITS % 2, v // PIECES, v % PIECES:v % PIECES + 1], bank(MAX_BANKS[u % len(MAX_BANKS)])[:, 0:w], X,
                                  ALU.max).then_inc(max_read, 1)

            def split_max(G, n):
                lev = [mlev[:, :, k, :] for k in range(LEVELS)]
                neg = negmax[:, :].rearrange("p (t h) -> p t h", t=TPC)
                res = nres[:, :].rearrange("p (t h) -> p t h", t=TPC)
                if n == 0:
                    dve.wait_ge(max_read, UNITS * (G + 1))
                    ins = dve.tensor_reduce(negmax[:, :], mpart[:, G % 2, :, :], X, ALU.max, negate=True)
                elif n == 1:
                    if G >= 1:
                        dve.wait_ge(maxT_ready, G)
                    ins = dve.tensor_copy(lev[0], neg)
                elif n == 2:
                    ins = dve.tensor_tensor(res, neg, lev[0], ALU.subtract)
                elif n == 3:
                    ins = dve.tensor_copy(lev[1], res)
                elif n == 4:
                    ins = dve.tensor_tensor(res, res, lev[1], ALU.subtract)
                else:
                    dve.tensor_copy(lev[2], res).then_inc(max_split, 1)
                if n < SPLIT_STEPS - 1:
                    link(ins)

            def divide(G):
                dve.wait_ge(den_ready, G + 1)
                num = bank(5).rearrange("p (t h w) -> p t h w", t=TPC, h=GROUP)
                link(dve.reciprocal(den_rec[:, :, :, :], num[:, :, :, C_DH:C_DH + 1]))
                if G >= GROUPS:
                    dve.wait_ge(attnT_ready, DK * (G // GROUPS))
                dve.tensor_tensor(attn[:, :, G % GROUPS, :, :], num[:, :, :, 0:C_DH],
                                  den_rec[:, :, :, :].broadcast_to([P, TPC, GROUP, C_DH]),
                                  ALU.mult).then_inc(attn_ready, 1)

            def add_residual(c, half, ready, read):
                k = 2 * c + half
                dve.wait_ge(ready, k + 1)
                at = TPC * c + 2 * half
                dve.tensor_tensor(x_sb[:, at:at + 2, :], bank(5).rearrange("p (t n) -> p t n", t=2),
                                  x_sb[:, at:at + 2, :], ALU.add).then_inc(read, 1)
                dve.wait_ge(read, k + 1)
                for q in range(2):
                    norm_stats(x_sb[:, at + q, :], 2 * half + q, None, None)

            def normalise(c, rsig, done):
                dve.wait_ge(rsig, c + 1)
                for t in range(TPC):
                    dve.tensor_scalar(x_sb[:, TPC * c + t, :], x_sb[:, TPC * c + t, :], meanvar[:, t, 0:1],
                                      rstd[:, t:t + 1], ALU.subtract, ALU.mult).then_inc(done, 1)

            def add_eps(sig):
                dve.tensor_scalar(var_eps[:, :], meanvar[:, :, 1], EPS, None, ALU.add).then_inc(sig, 1)

            def chunk_tail(c, n):
                if n < 10:
                    half, m = divmod(n, 5)
                    q, k = 2 * half + (m - 1) // 2, 2 * c + half
                    if m == 0:
                        dve.wait_ge(co_ready, k + 1)
                        at = TPC * c + 2 * half
                        dve.tensor_tensor(x_sb[:, at:at + 2, :], bank(5).rearrange("p (t n) -> p t n", t=2),
                                          x_sb[:, at:at + 2, :], ALU.add).then_inc(co_read, 1)
                        dve.wait_ge(co_read, k + 1)
                    elif m % 2 == 1:
                        link(dve.bn_stats(stats[:, q, :], x_sb[:, TPC * c + q, :]))
                    else:
                        link(dve.bn_aggr(meanvar[:, q, :], stats[:, q, :]))
                elif n == 10:
                    add_eps(c_var)
                else:
                    t = n - 11
                    if t == 0:
                        dve.wait_ge(c_rstd, c + 1)
                    dve.tensor_scalar(x_sb[:, TPC * c + t, :], x_sb[:, TPC * c + t, :], meanvar[:, t, 0:1],
                                      rstd[:, t:t + 1], ALU.subtract, ALU.mult).then_inc(x2_ready, 1)

            def reads(lo, hi, tail_chunk=None, tail_at=0):
                for u in range(lo, hi):
                    read_max(u)
                    if tail_chunk is not None and tail_at + u - lo < 11 + TPC:
                        chunk_tail(tail_chunk, tail_at + u - lo)
                    if u >= UNITS and u % UNITS < SPLIT_STEPS:
                        split_max(u // UNITS - 1, u % UNITS)
                    if u == CHUNKS * GROUPS * UNITS - 1:
                        for step in range(SPLIT_STEPS):
                            split_max(u // UNITS, step)

            def wide(ap, n):
                return ap.rearrange("p (t o) -> p t o", o=1).broadcast_to([P, n, EXPERTS])

            def gate_softmax(call, lo, hi):
                n = hi - lo
                one, work, p = small[:, 0:n], gate_work[:, lo:hi, :], probs[:, lo:hi, :]
                dve.wait_ge(logits_copied, hi // TPC)
                link(dve.tensor_reduce(one, logits[:, lo:hi, :], X, ALU.max))
                dve.tensor_tensor(work, logits[:, lo:hi, :], wide(one, n), ALU.subtract).then_inc(gate_centred, 1)
                dve.wait_ge(gate_exp, call)
                link(dve.tensor_reduce(one, work, X, ALU.add))
                link(dve.reciprocal(one, one))
                link(dve.tensor_tensor(p, work, wide(one, n), ALU.mult))

            def gate_choice(call, lo, hi):
                n = hi - lo
                one, two = small[:, 0:n], small[:, 16:16 + n]
                work, equal, count, p = (x[:, lo:hi, :] for x in (gate_work, gate_equal, gate_count, probs))

                def flat(ap):
                    return ap.rearrange("p t e -> p (t e)")

                for t in range(lo, hi):
                    ins = dve.max(top8[:, t, :], probs[:, t, :])
                link(ins)
                fourth = top8[:, lo:hi, TOPK - 1:TOPK].broadcast_to([P, n, EXPERTS])
                link(dve.tensor_tensor(equal, p, fourth, ALU.is_equal))
                link(dve.tensor_tensor(work, p, fourth, ALU.is_gt))
                link(dve.tensor_reduce(one, work, X, ALU.add))
                link(dve.tensor_scalar(one, one, -1.0, float(TOPK), ALU.mult, ALU.add))
                dve.wait_ge(zero_ready, 1)
                link(dve.tensor_tensor_scan(flat(count), flat(equal), flat(zero_gate[:, lo:hi, :]), 0.0,
                                            ALU.add, ALU.add))
                link(dve.tensor_tensor(two[:, 1:n], one[:, 1:n], count[:, 0:n - 1, EXPERTS - 1], ALU.add))
                link(dve.tensor_copy(two[:, 0:1], one[:, 0:1]))
                link(dve.tensor_tensor(count, count, wide(two, n), ALU.is_le))
                link(dve.tensor_tensor(equal, equal, count, ALU.mult))
                link(dve.tensor_tensor(work, work, equal, ALU.add))
                link(dve.tensor_tensor(p, p, work, ALU.mult))
                link(dve.tensor_reduce(one, p, X, ALU.add))
                link(dve.reciprocal(one, one))
                link(dve.tensor_tensor(p, p, wide(one, n), ALU.mult))
                link(dve.tensor_copy(gate_parts[:, lo:hi, 0, :], p))
                dve.tensor_tensor(gate_parts[:, lo:hi, 1, :], p, gate_parts[:, lo:hi, 0, :].bitcast(F32),
                                  ALU.subtract).then_inc(gate_ready, 1)

            dve.wait_ge(x1_biased, TILES)
            reads(0, units_until(-1))
            for s in range(STEPS):
                G, kt = divmod(s, KT)
                c, g = divmod(G, GROUPS)
                lo, hi = units_until(s - 1), units_until(s)
                if g == 0 and c >= 1 and kt >= 7:
                    reads(lo, hi, c - 1, lo - units_until(s - kt + 6))
                else:
                    reads(lo, hi)
                if kt == 3 and G >= 1:
                    divide(G - 1)
                if G == CHUNKS * GROUPS - 1 and kt == 4:
                    gate_softmax(1, 0, GATE_FIRST)
                    gate_choice(1, 0, GATE_FIRST)

            for c in range(CHUNKS):
                for e in range(FFN):
                    i = FFN * c + e
                    b = 2 * (i % 2)
                    dve.wait_ge(h_ready, i + 1)
                    if i >= 1:
                        dve.wait_ge(act_ready, i)
                    if e < EXPERTS:
                        dve.wait_ge(blend_copied, EXPERTS * c + e + 1)
                        ins = dve.tensor_tensor(weighted[:, :], bank(b + 1), blend_s[:, :], ALU.mult)
                    else:
                        ins = dve.tensor_scalar(weighted[:, :], bank(b + 1), 0.5, None, ALU.mult)
                    ins.then_inc(weighted_ready, 1)
                    dve.wait_ge(tanh_ready, i + 1)
                    dve.scalar_tensor_tensor(out=silu_h[:, :], in0=tanh_h[:, i % 2, :], scalar=1.0, in1=bank(b),
                                             op0=ALU.add, op1=ALU.mult).then_inc(h_read, 1)
                    dve.wait_ge(weighted_ready, i + 1)
                    dve.wait_ge(h_read, i + 1)
                    if i >= 2:
                        dve.wait_ge(act_lo_ready, i - 1)
                    dve.tensor_tensor(act_h[:, i % 2, :], silu_h[:, :], weighted[:, :], ALU.mult).then_inc(act_ready, 1)
                    dve.wait_ge(act_hi_ready, i + 1)
                    if i >= 2:
                        dve.wait_ge(act_done, i - 1)
                    dve.tensor_tensor(act_lo[:, i % 2, :], act_h[:, i % 2, :], act_hi[:, i % 2, :].bitcast(F32),
                                      ALU.subtract).then_inc(act_lo_ready, 1)
                    if i == 0:
                        divide(CHUNKS * GROUPS - 1)
                    if i == 3:
                        for n_tail in range(5):
                            chunk_tail(CHUNKS - 1, n_tail)
                    if i == 4:
                        for n_tail in range(5, 11):
                            chunk_tail(CHUNKS - 1, n_tail)
                    if i == 5:
                        for n_tail in range(11, 11 + TPC):
                            chunk_tail(CHUNKS - 1, n_tail)
                    if i == 9:
                        gate_softmax(2, GATE_FIRST, TILES)
                    if i == 10:
                        gate_choice(2, GATE_FIRST, TILES)
                    if c >= 1 and e in (3, 5):
                        add_residual(c - 1, e // 2 - 1, ffnN_ready, ffnN_read)
                    if c >= 1 and e == 5:
                        add_eps(d_var)
                    if c >= 1 and e == 6:
                        normalise(c - 1, d_rstd, out_ready)
            for half in range(2):
                add_residual(CHUNKS - 1, half, ffnN_ready, ffnN_read)
            add_eps(d_var)
            normalise(CHUNKS - 1, d_rstd, out_ready)


def _launch_arrays(i):
    import numpy as np

    def arr(x):
        return np.ascontiguousarray(x)

    n = {k: np.asarray(v) for k, v in i.items()}
    out = {
        "x": arr(n["x"][0]), "xT": arr(n["x"][0].T), "ctxT": arr(n["ctx_1024"][0].T),
        "bq2": arr(n["L0_xattn_bq"].reshape(DK, P).T), "bk2": arr(n["L0_xattn_bk"].reshape(DK, P).T),
        "gateT": arr(n["L0_ffn_gate_w"].T),
        "w1T": arr(n["L0_ffn_w1"].transpose(2, 0, 1)), "w3T": arr(n["L0_ffn_w3"].transpose(2, 0, 1)),
        "w2T": arr(n["L0_ffn_w2"].transpose(2, 0, 1)),
        "sw1T": arr(n["L0_ffn_sw1"].T), "sw3T": arr(n["L0_ffn_sw3"].T), "sw2T": arr(n["L0_ffn_sw2"].T),
    }
    for k in ("L0_attn_Wq", "L0_attn_Wk", "L0_attn_Wv", "L0_attn_Wo", "L0_attn_bo", "L0_xattn_Wq",
              "L0_xattn_Wk", "L0_xattn_Wv", "L0_xattn_bv", "L0_xattn_Wo", "L0_xattn_bo"):
        out[k] = arr(n[k])
    return out


def kernel(**inputs):
    import numpy as np
    import concourse.bacc as bacc
    from concourse.bass_utils import run_bass_kernel_spmd

    nc = bacc.Bacc("TRN2", target_bir_lowering=False, num_devices=1, dynamic_dma_scratch_size=1024)
    given = _launch_arrays(inputs)
    arrays = {f"in_{k}": v for k, v in given.items()}
    aps = {k: nc.dram_tensor(f"in_{k}", v.shape, mybir.dt.from_np(v.dtype), kind="ExternalInput").ap()
           for k, v in given.items()}
    out = nc.dram_tensor("out_dram", (SEQ, DIM), F32, kind="ExternalOutput").ap()
    decoder_layer(nc, aps, out)
    got = run_bass_kernel_spmd(nc, [arrays], core_ids=[0]).results[0]["out_dram"]
    return np.asarray(got).reshape(1, SEQ, DIM)
```
